# Optimizing a Trainium2 kernel written in Bass

```python
import numpy as np
import jax
import jax.numpy as jnp

def _softmax(x, axis=-1):
    return jax.nn.softmax(x, axis=axis)

def _gelu(x):
    return jax.nn.gelu(x, approximate=True)

def _silu(x):
    return jax.nn.silu(x)

def _sigmoid(x):
    return jax.nn.sigmoid(x)

def _layernorm(x, axis=-1, eps=1e-05):
    m = jnp.mean(x, axis=axis, keepdims=True)
    v = jnp.var(x, axis=axis, keepdims=True)
    return (x - m) / jnp.sqrt(v + eps)

def _scatter_add(tgt, idx, src, axis=0):
    return tgt.at[idx].add(src)

def _segment_sum(src, seg, n):
    return jax.ops.segment_sum(src, seg, n)
kernel_name = 'mk_adaln_ffn_d2_seqx_r8_6239af'

def setup_inputs(seed: int=0):
    np.random.seed(seed)
    _w = jnp.asarray

    def _rec_inputs():
        import jax
        import jax.numpy as jnp
        _rk = jax.random.key(seed)
        x = -0.000125 + 0.9999 * jax.random.normal(jax.random.fold_in(_rk, 1), (128, 32, 512), jnp.float32)
        _lenS = 32 - jax.random.randint(jax.random.fold_in(_rk, 7), (128,), 0, max(1, 32 // 4) + 1, jnp.int32)
        _lenS2 = 32 - jax.random.randint(jax.random.fold_in(_rk, 8), (128,), 0, max(1, 32 // 4) + 1, jnp.int32)
        cond_128 = 0.0061147 + 1.02565 * jax.random.normal(jax.random.fold_in(_rk, 11), (128, 128), jnp.float32)
        fside_S_0 = -0.022604 + 0.987366 * jax.random.normal(jax.random.fold_in(_rk, 12), (32,), jnp.float32)
        return (x, cond_128, fside_S_0)
    x, cond_128, fside_S_0 = _rec_inputs()

    def _L0_cond_setup():
        import jax, jax.numpy as jnp
        import numpy as np
        K = 8
        T = 1.0
        D_EMBD = 128
        IN_C = 32
        OUT_C = 32
        BS = 32
        H = 512
        HID = 128
        key = jax.random.key(seed)
        ks = jax.random.split(key, 10)
        s = lambda fan_in: 1.0 / np.sqrt(fan_in)
        return {'x': jax.random.normal(ks[0], (BS, IN_C, H), dtype=jnp.float32), 'embedding': jax.random.normal(ks[1], (BS, D_EMBD), dtype=jnp.float32), 'W0': jax.random.normal(ks[2], (D_EMBD, HID), dtype=jnp.float32) * s(D_EMBD), 'b0': jnp.zeros((HID,), dtype=jnp.float32), 'W1': jax.random.normal(ks[3], (HID, HID), dtype=jnp.float32) * s(HID), 'b1': jnp.zeros((HID,), dtype=jnp.float32), 'W2': jax.random.normal(ks[4], (HID, K), dtype=jnp.float32) * s(HID), 'b2': jnp.zeros((K,), dtype=jnp.float32), 'weight': jax.random.normal(ks[5], (K, OUT_C, IN_C, 1), dtype=jnp.float32) * s(IN_C), 'bias_k': jax.random.normal(ks[6], (K, OUT_C), dtype=jnp.float32) * 0.1}
    _L0_cond_all = _L0_cond_setup()
    _L0_cond_in = {k: v for k, v in _L0_cond_all.items() if k in ('W0', 'b0', 'W1', 'b1', 'W2', 'b2', 'weight', 'bias_k')}
    del _L0_cond_all

    def _L0_ffn_setup():
        import jax, jax.numpy as jnp
        import numpy as np
        LORA_R = 16
        SCALE = 16.0 / np.sqrt(16.0)
        NUM_EXPERTS = 4
        TOP_K = 2
        IN_F = 512
        OUT_F = 512
        key = jax.random.key(seed)
        k_x, k_a, k_b, k_r = jax.random.split(key, 4)
        x = jax.random.normal(k_x, (2, 256, IN_F), dtype=jnp.float32)
        A = jax.random.normal(k_a, (NUM_EXPERTS, LORA_R, IN_F), dtype=jnp.float32) * (1.0 / np.sqrt(IN_F))
        B = jax.random.normal(k_b, (NUM_EXPERTS, OUT_F, LORA_R), dtype=jnp.float32) * 0.02
        Wr = jax.random.normal(k_r, (NUM_EXPERTS, IN_F), dtype=jnp.float32) * 0.02
        return {'x': x, 'A': A, 'B': B, 'Wr': Wr}
    _L0_ffn_all = _L0_ffn_setup()
    _L0_ffn_in = {k: v for k, v in _L0_ffn_all.items() if k in ('A', 'B', 'Wr')}
    del _L0_ffn_all

    def _L1_cond_setup():
        import jax, jax.numpy as jnp
        import numpy as np
        from jax import lax
        N, C_IN, L = (32, 32, 512)
        C_OUT, K, GROUPS = (32, 9, 4)
        C_DIM, PAD, STRIDE = (128, 4, 1)
        key = jax.random.key(seed)
        k1, k2, k3, k4, k5 = jax.random.split(key, 5)
        x = jax.random.normal(k1, (N, C_IN, L), dtype=jnp.float32)
        c = jax.random.normal(k2, (N, C_DIM), dtype=jnp.float32)
        weight = jax.random.normal(k3, (C_OUT, C_IN // GROUPS, K), dtype=jnp.float32)
        c_weight = jax.random.normal(k4, (C_OUT, C_DIM), dtype=jnp.float32)
        bias = jax.random.normal(k5, (C_OUT,), dtype=jnp.float32)
        return {'x': x, 'c': c, 'weight': weight, 'c_weight': c_weight, 'bias': bias}
    _L1_cond_all = _L1_cond_setup()
    _L1_cond_in = {k: v for k, v in _L1_cond_all.items() if k in ('weight', 'c_weight')}
    del _L1_cond_all

    def _L1_ffn_setup():
        import jax, jax.numpy as jnp
        import numpy as np
        B, S, IN, OUT = (4, 256, 512, 512)
        E, K, R = (8, 2, 16)
        CAP_FACTOR = 3.0
        ALPHA = 1.0 / R
        LN_EPS = 1e-05
        key = jax.random.key(seed)
        ks = jax.random.split(key, 6)
        return {'x': jax.random.normal(ks[0], (B, S, IN), dtype=jnp.float32), 'weight': jax.random.normal(ks[1], (OUT, IN), dtype=jnp.float32) * 0.02, 'lora_A': jax.random.normal(ks[2], (E, IN, R), dtype=jnp.float32) / np.sqrt(R), 'lora_B': jax.random.normal(ks[3], (E, R, OUT), dtype=jnp.float32) * 0.02, 'gw1': jax.random.normal(ks[4], (4 * E, IN), dtype=jnp.float32) * 0.02, 'gb1': jnp.zeros((4 * E,), dtype=jnp.float32), 'ln_gamma': jnp.ones((4 * E,), dtype=jnp.float32), 'ln_beta': jnp.zeros((4 * E,), dtype=jnp.float32), 'gw2': jax.random.normal(ks[5], (E, 4 * E), dtype=jnp.float32) * 0.02, 'gb2': jnp.zeros((E,), dtype=jnp.float32)}
    _L1_ffn_all = _L1_ffn_setup()
    _L1_ffn_in = {k: v for k, v in _L1_ffn_all.items() if k in ('weight', 'lora_A', 'lora_B', 'gw1', 'gb1', 'ln_gamma', 'ln_beta', 'gw2', 'gb2')}
    del _L1_ffn_all
    return {'x': x, 'cond_128': cond_128, 'fside_S_0': fside_S_0, 'L0_cond_W0': _L0_cond_in['W0'], 'L0_cond_b0': _L0_cond_in['b0'], 'L0_cond_W1': _L0_cond_in['W1'], 'L0_cond_b1': _L0_cond_in['b1'], 'L0_cond_W2': _L0_cond_in['W2'], 'L0_cond_b2': _L0_cond_in['b2'], 'L0_cond_weight': _L0_cond_in['weight'], 'L0_cond_bias_k': _L0_cond_in['bias_k'], 'L0_ffn_A': _L0_ffn_in['A'], 'L0_ffn_B': _L0_ffn_in['B'], 'L0_ffn_Wr': _L0_ffn_in['Wr'], 'L1_cond_weight': _L1_cond_in['weight'], 'L1_cond_c_weight': _L1_cond_in['c_weight'], 'L1_ffn_weight': _L1_ffn_in['weight'], 'L1_ffn_lora_A': _L1_ffn_in['lora_A'], 'L1_ffn_lora_B': _L1_ffn_in['lora_B'], 'L1_ffn_gw1': _L1_ffn_in['gw1'], 'L1_ffn_gb1': _L1_ffn_in['gb1'], 'L1_ffn_ln_gamma': _L1_ffn_in['ln_gamma'], 'L1_ffn_ln_beta': _L1_ffn_in['ln_beta'], 'L1_ffn_gw2': _L1_ffn_in['gw2'], 'L1_ffn_gb2': _L1_ffn_in['gb2']}

def reference(x, cond_128, fside_S_0, L0_cond_W0, L0_cond_b0, L0_cond_W1, L0_cond_b1, L0_cond_W2, L0_cond_b2, L0_cond_weight, L0_cond_bias_k, L0_ffn_A, L0_ffn_B, L0_ffn_Wr, L1_cond_weight, L1_cond_c_weight, L1_ffn_weight, L1_ffn_lora_A, L1_ffn_lora_B, L1_ffn_gw1, L1_ffn_gb1, L1_ffn_ln_gamma, L1_ffn_ln_beta, L1_ffn_gw2, L1_ffn_gb2):
    import jax
    import jax.numpy as jnp

    def _L0_cond_ref(x, embedding, W0, b0, W1, b1, W2, b2, weight, bias_k):
        import jax, jax.numpy as jnp
        import numpy as np
        K = 8
        T = 1.0
        D_EMBD = 128
        IN_C = 32
        OUT_C = 32
        BS = 32
        H = 512
        HID = 128
        h = jax.nn.gelu(embedding @ W0 + b0, approximate=False)
        h = jax.nn.gelu(h @ W1 + b1, approximate=False)
        att = jax.nn.softmax((h @ W2 + b2) / T, axis=-1)
        agg_w = jnp.einsum('bk,koi->boi', att, weight[..., 0])
        agg_b = att @ bias_k
        out = jnp.einsum('boi,bih->boh', agg_w, x) + agg_b[:, :, None]
        return out

    def _L0_ffn_ref(x, A, B, Wr):
        import jax, jax.numpy as jnp
        import numpy as np
        LORA_R = 16
        SCALE = 16.0 / np.sqrt(16.0)
        NUM_EXPERTS = 4
        TOP_K = 2
        IN_F = 512
        OUT_F = 512
        orig_shape = x.shape
        flat = x.reshape(-1, orig_shape[-1])
        logits = flat @ Wr.T
        topk_vals, topk_idx = jax.lax.top_k(logits, TOP_K)
        T = flat.shape[0]
        neg_inf = jnp.finfo(logits.dtype).min
        sparse = jnp.full_like(logits, neg_inf)
        rows = jnp.arange(T)[:, None]
        sparse = sparse.at[rows, topk_idx].set(topk_vals)
        gates = jax.nn.softmax(sparse, axis=-1)
        mid = jnp.einsum('tf,erf->ter', flat, A)
        all_deltas = jnp.einsum('ter,eor->teo', mid, B) * SCALE
        delta = jnp.sum(gates[:, :, None] * all_deltas, axis=1)
        return delta.reshape(*orig_shape[:-1], -1)

    def _L1_cond_ref(x, c, weight, c_weight, bias):
        import jax, jax.numpy as jnp
        import numpy as np
        from jax import lax
        N, C_IN, L = (32, 32, 512)
        C_OUT, K, GROUPS = (32, 9, 4)
        C_DIM, PAD, STRIDE = (128, 4, 1)
        out = lax.conv_general_dilated(x, weight, window_strides=(STRIDE,), padding=[(PAD, PAD)], dimension_numbers=('NCH', 'OIH', 'NCH'), feature_group_count=GROUPS)
        ctx = jnp.einsum('nd,od->no', c, c_weight)
        out = out + ctx[:, :, None] + bias[None, :, None]
        return out

    def _L1_ffn_ref(x, weight, lora_A, lora_B, gw1, gb1, ln_gamma, ln_beta, gw2, gb2):
        import jax, jax.numpy as jnp
        import numpy as np
        B, S, IN, OUT = (4, 256, 512, 512)
        E, K, R = (8, 2, 16)
        CAP_FACTOR = 3.0
        ALPHA = 1.0 / R
        LN_EPS = 1e-05
        orig_shape = x.shape
        xf = x.reshape(-1, orig_shape[-1])
        N = xf.shape[0]
        capacity = int(CAP_FACTOR * N / E)
        h = xf @ gw1.T + gb1
        mu = jnp.mean(h, axis=-1, keepdims=True)
        var = jnp.mean((h - mu) ** 2, axis=-1, keepdims=True)
        h = (h - mu) * jax.lax.rsqrt(var + LN_EPS) * ln_gamma + ln_beta
        h = jax.nn.relu(h)
        gates = h @ gw2.T + gb2
        top_v, top_i = jax.lax.top_k(gates, K)
        top_g = jax.nn.softmax(top_v, axis=-1)
        onehot = (top_i[..., None] == jnp.arange(E)).astype(xf.dtype)
        counts = onehot.sum(axis=0)
        allowed = (counts <= capacity).astype(xf.dtype)
        w = jnp.einsum('nke,nk,ke->ne', onehot, top_g, allowed)
        main = xf @ weight.T
        tmp = jnp.einsum('ni,eir->enr', xf, lora_A)
        tmp = tmp * w.T[:, :, None]
        lora = jnp.einsum('enr,ero->no', tmp, lora_B) * ALPHA
        out = main + lora
        return out.reshape(*orig_shape[:-1], weight.shape[0])
    x = x + _L0_ffn_ref(_L0_cond_ref(x, cond_128, L0_cond_W0, L0_cond_b0, L0_cond_W1, L0_cond_b1, L0_cond_W2, L0_cond_b2, L0_cond_weight, L0_cond_bias_k), L0_ffn_A, L0_ffn_B, L0_ffn_Wr)
    x = x + _L1_ffn_ref(_L1_cond_ref(x, cond_128, L1_cond_weight, L1_cond_c_weight, fside_S_0), L1_ffn_weight, L1_ffn_lora_A, L1_ffn_lora_B, L1_ffn_gw1, L1_ffn_gb1, L1_ffn_ln_gamma, L1_ffn_ln_beta, L1_ffn_gw2, L1_ffn_gb2)
    return x

_drawn_inputs = setup_inputs


def setup_inputs(seed=0):
    import zlib

    import numpy as np

    out = dict(_drawn_inputs(seed))
    spreads = {'L0_cond_b0': (0.0, 0.8),
     'L0_cond_b1': (0.0, 0.572),
     'L0_cond_b2': (0.0, 0.675),
     'L1_ffn_gb1': (0.0, 2.0),
     'L1_ffn_ln_gamma': (1.0, 0.6),
     'L1_ffn_ln_beta': (0.0, 1.643),
     'L1_ffn_gb2': (0.0, 0.1)}
    factors = {'L0_cond_bias_k': 5.209}
    for name, (base, spread) in spreads.items():
        noise = np.random.default_rng([zlib.crc32(name.encode()), seed]).standard_normal(out[name].shape)
        drawn = base * np.exp(spread * noise) if base else spread * noise
        out[name] = jnp.asarray(drawn.astype(out[name].dtype))
    for name, factor in factors.items():
        out[name] = (out[name] * factor).astype(out[name].dtype)
    return out
```

```python
import concourse.bass as bass
from concourse import mybir
from contextlib import ExitStack



def adaln_ffn_kernel(nc: bass.Bass, x, cond, fside, w0, b0, w1, b1, w2, b2, mixw, mixb, ffa, ffb, ffr,
                     convw, ctxw, wmain, lora_a, lora_b, gw1, gb1, gamma, beta, gw2, gb2, out):
    fp32 = mybir.dt.float32
    fp32r = mybir.dt.float32r
    ALU = mybir.AluOpType
    ACT = mybir.ActivationFunctionType
    AXX = mybir.AxisListType.X

    P = 128
    NB, C, H = x.shape
    K0 = mixw.shape[0]
    E0, R0 = ffa.shape[0], ffa.shape[1]
    ER0 = E0 * R0
    UC = ER0 + E0
    SCALE0 = 16.0 / float(R0) ** 0.5
    E1, R1 = lora_a.shape[0], lora_a.shape[2]
    ER1 = E1 * R1
    G1 = gw1.shape[0]
    GC = G1 + ER1
    TAPS = convw.shape[2]
    CG = convw.shape[1]
    CAPACITY = int(3.0 * NB * C / E1)
    ALPHA = 1.0 / R1
    EPS = 1e-05
    BT = P // C
    NT = 4
    NS = NB // (BT * NT)
    Q = 4
    M = H // Q
    HC = H // P
    SH = 3
    ST = NT * H

    x_v = x.rearrange("(s t b) c h -> s (b c) t h", t=NT, b=BT)
    out_v = out.rearrange("(n b) c h -> n (b c) h", b=BT)

    ctx = ExitStack()
    with ctx:
        def sb(name, shape, dt=fp32):
            return ctx.enter_context(nc.sbuf_tensor(name, shape, dt))

        def sem(name):
            return ctx.enter_context(nc.semaphore(name))

        def row(v, axis, n):
            v = v.unsqueeze(axis)
            shape = list(v.shape)
            shape[axis] = n
            return v.broadcast_to(shape)

        def wait(eng, s, value):
            if not isinstance(value, int) or value > 0:
                eng.wait_ge(s, value)

        y_all = sb("y_all", [P, NS * ST])
        tmp_all = sb("tmp_all", [P, NS * NT * ER1])
        wst_all = sb("wst_all", [P, NS * NT, 2, E1])
        mix_all = sb("mix_all", [P, C, NB])
        wt_hi = sb("wt_hi", [P, Q, H], fp32r)
        wt_lo = sb("wt_lo", [P, Q, H], fp32r)
        xs = [sb(f"xs{i}", [P, NT, H]) for i in range(2)]
        xT = sb("xT", [P, NT, HC, P])
        xp = [sb(f"xp{i}", [P, BT, NT, M + 2]) for i in range(2)]
        o1 = [sb(f"o1_{i}", [P, Q, BT, C]) for i in range(2)]
        o1h = [sb(f"o1h{i}", [P, Q, P], fp32r) for i in range(2)]
        o1l = [sb(f"o1l{i}", [P, Q, P], fp32r) for i in range(2)]
        bias = [sb(f"bias{i}", [P, NT, BT, C]) for i in range(2)]
        mixbd = sb("mixbd", [P, NT, BT, C])
        mixbias = sb("mixbias", [P, NS * NT])
        pm = sb("pm", [P, HC, UC])
        rs = sb("rs", [P, UC])
        b_hi = sb("b_hi", [P, H], fp32r)
        b_lo = sb("b_lo", [P, H], fp32r)
        ga = sb("ga", [P, Q, GC])
        cw = sb("cw", [P, SH, Q, C])
        lb_hi = sb("lb_hi", [P, H], fp32r)
        lb_lo = sb("lb_lo", [P, H], fp32r)
        gw2bd = sb("gw2bd", [P, NT, E1])
        ident = sb("ident", [P, P])
        ones = sb("ones", [P, P])
        u_sb = sb("u_sb", [P, NT, UC])
        vb = sb("vb", [P, NT, UC])
        v = sb("v", [P, NT, UC])
        gms = sb("gms", [P, NT, 2, ER0])
        gm = sb("gm", [P, NT, ER0])
        gmT = sb("gmT", [P, NT * P], fp32r)
        hs = sb("hs", [P, NT, G1])
        ha = sb("ha", [P, NT, G1])
        hb = sb("hb", [P, NT, G1])
        hr = sb("hr", [P, NT, G1])
        hT = sb("hT", [P, P])
        gb1_b = sb("gb1_b", [P, G1])
        gamma_b = sb("gamma_b", [P, G1])
        beta_b = sb("beta_b", [P, G1])
        gb2_b = sb("gb2_b", [P, E1])
        repmask = sb("repmask", [P, BT])
        upper = sb("upper", [P, E1, E1])
        sel0 = sb("sel0", [P, E0])
        sel1 = sb("sel1", [P, 2, E1])
        mhalf = sb("mhalf", [P, NT])
        small = sb("small", [P, 24, NT])
        sc0 = sb("sc0", [P, 8, NT, E0])
        pair0 = sb("pair0", [P, 2, NT, E0, E0])
        sc1 = sb("sc1", [P, 6, NT, E1])
        oh = sb("oh", [P, NT, 2, E1])
        exs1 = sb("exs1", [P, NT, 2, E1])
        pair1 = sb("pair1", [P, 2, NT, E1, E1])
        cnt = sb("cnt", [P, 2, E1])
        cnt1 = sb("cnt1", [P, 2, E1])
        allowed = sb("allowed", [P, 2, E1])

        at = [2 * ST]

        def early(parts, shape):
            n = 1
            for d in shape:
                n *= d
            a = y_all[0:parts, at[0]:at[0] + n]
            at[0] += n
            assert at[0] <= NS * ST
            if len(shape) == 1:
                return a
            names = "abcd"[:len(shape)]
            return a.rearrange(f"p ({' '.join(names)}) -> p {' '.join(names)}",
                               **{k: d for k, d in zip(names[1:], shape[1:])})

        wn = early(P, [HC, H])
        wk = early(K0, [C, BT, C])
        bn = early(P, [HC, 2, ER0])
        aw = early(UC, [H])
        gw1n = early(G1, [H])
        gw2n = early(E1, [NT, G1])
        lbn = early(P, [H])
        condn = early(P, [P])
        w0n = early(P, [P])
        w1n = early(P, [P])
        condT = early(P, [P])
        h1 = early(P, [P])
        h2 = early(P, [P])
        w2n = early(P, [K0])
        b0c = early(P, [1])
        b1c = early(P, [1])
        b2b = early(P, [K0])
        mbn = early(K0, [BT, C])
        ctxn = early(C, [P])
        ctxT = early(P, [C])
        ctxb = early(P, [C])
        fsb = early(P, [C])
        cwt = early(P, [CG, TAPS])
        att = early(P, [K0])
        atte = early(P, [K0])
        attT = early(K0, [P])
        gq = early(P, [BT, C // CG])
        gmask = early(P, [C // CG])
        sm = early(P, [4])

        def pb(name):
            return ctx.enter_context(nc.psum_tensor(name, [P, 512], fp32))

        ps_a = [pb("ps_a0"), pb("ps_a1")]
        ps_t = pb("ps_t")
        ps_v = pb("ps_v")
        ps_d = [pb("ps_d0"), pb("ps_d1")]
        ps_c = pb("ps_c")
        ps_g = pb("ps_g")

        cbias = nc.dram_tensor("cbias", (NB * C,), fp32).ap()

        s_x = [sem(f"x_loaded{i}") for i in range(2)]
        s_bias = [sem(f"bias_loaded{i}") for i in range(2)]
        s_ld = {n: sem(f"ld_{n}") for n in ("cond", "mlp", "aw", "mixw", "mixb", "bn", "w", "gate", "ctx", "conv",
                                            "lora", "rows")}
        s_cbias = sem("cbias_stored")
        s_id = sem("ident_steps")
        s_const = sem("consts_ready")
        s_zero = sem("zeros_ready")
        names = ("condT", "pm", "h1", "ctxT", "b", "h2", "gw1", "att", "ctx", "rs", "attT")
        s_sp = {n: sem(f"setup_ps_{n}") for n in names}
        s_ss = {n: sem(f"setup_sb_{n}") for n in names}
        s_wps, s_whi, s_wlo = sem("w_ps"), sem("w_hi"), sem("w_lo")
        s_mps, s_msb = sem("mix_ps"), sem("mix_sb")
        s_mbps, s_mbsb = sem("mixbias_ps"), sem("mixbias_sb")
        s_cw = sem("convw_ready")
        s_lb = sem("lora_b_split")
        s_sc, s_sd = sem("setup_chain_act"), sem("setup_chain_dve")
        s_attd, s_atte = sem("att_shifted"), sem("att_exp")

        s_xtp, s_xt = sem("xT_ps"), sem("xT_copied")
        s_up, s_u = sem("u_ps"), sem("u_copied")
        s_bd, s_vb = sem("mixbd_ready"), sem("vbias_ready")
        s_vp, s_v = sem("v_ps"), sem("v_ready")
        s_df0, s_ex0 = sem("gate0_shifted"), sem("gate0_exp")
        s_c0 = sem("gate0_chain")
        s_gm, s_gtp, s_gt = sem("gm_ready"), sem("gmT_ps"), sem("gmT_copied")
        s_dp, s_x1 = sem("delta_ps"), sem("x1_ready")
        s_xpd, s_xpa = sem("xp_dve"), sem("xp_act")
        s_cp, s_o1 = sem("conv_ps"), sem("o1_ready")
        s_o1h, s_o1l = sem("o1_hi"), sem("o1_lo")
        s_gp, s_g = sem("ga_ps"), sem("ga_copied")
        s_mp, s_y = sem("main_ps"), sem("y_ready")
        s_c1 = sem("norm_chain")
        s_var, s_rstd = sem("var_ready"), sem("rstd_ready")
        s_h, s_htp, s_ht = sem("hidden_ready"), sem("hT_ps"), sem("hT_copied")
        s_rp, s_r = sem("router_ps"), sem("router_read")
        s_df1, s_ex1 = sem("gate1_shifted"), sem("gate1_exp")
        s_c2 = sem("gate1_chain")
        s_cnt, s_cntp, s_w = sem("counts_ready"), sem("counts_ps"), sem("weights_ready")
        s_c3 = sem("allowed_chain")
        s_lt, s_ltp = sem("weighted"), sem("weighted_ps")
        s_lth, s_ltl = sem("weightedT_hi"), sem("weightedT_lo")
        s_lp, s_yo = sem("lora_ps"), [sem(f"out_ready{i}") for i in range(NT)]
        s_out = [sem(f"out_stored{i}") for i in range(NT)]

        ltw = xs[0]
        ltw_v = xs[0][:, 0, :].rearrange("p (t e r) -> p t e r", t=NT, e=E1)
        lt_hi = sb("lt_hi", [P, NT * P], fp32r)
        lt_lo = sb("lt_lo", [P, NT * P], fp32r)
        yo = [xT[:, t, :, :].rearrange("p c m -> p (c m)") for t in range(NT)]
        ps_l = [ps_d[0], ps_d[1], ps_c, ps_g]

        def chain(eng, s, base):
            n = [0]

            def link(ins):
                n[0] += 1
                ins.then_inc(s, 1)
                eng.wait_ge(s, base + n[0])
            return link, n

        N_C0, N_C1, N_C2 = 13, 9, 14

        def supertiles(eng, step):
            for s in range(-2, 2):
                step(s, s % 2, s // 2)
            with eng.Fori(1, NS // 2 - 1) as k:
                step(k * 2, 0, k)
                step(k * 2 + 1, 1, k)
            step(NS - 2, 0, NS // 2 - 1)
            step(NS - 1, 1, NS // 2 - 1)

        def has(s, ahead):
            return not isinstance(s, int) or 0 <= s + ahead < NS

        block = ctx.enter_context(nc.Block())

        @block.sync
        def _(sp):
            sp.dma_start(condn, cond).then_inc(s_ld["cond"], 16)
            sp.dma_start(w0n, w0).then_inc(s_ld["mlp"], 16)
            sp.dma_start(b0c, b0.rearrange("(p a) -> p a", a=1)).then_inc(s_ld["mlp"], 16)
            sp.dma_start(w1n, w1).then_inc(s_ld["mlp"], 16)
            sp.dma_start(b1c, b1.rearrange("(p a) -> p a", a=1)).then_inc(s_ld["mlp"], 16)
            sp.dma_start(w2n, w2).then_inc(s_ld["mlp"], 16)
            sp.dma_start(b2b, b2.partition_broadcast(P)).then_inc(s_ld["mlp"], 16)
            sp.dma_start(aw[0:ER0], ffa.rearrange("e r h -> (e r) h")).then_inc(s_ld["aw"], 16)
            sp.dma_start(aw[ER0:UC], ffr).then_inc(s_ld["aw"], 16)
            for i in range(2):
                sp.dma_start(xs[i][:, :, :], x_v[i]).then_inc(s_x[i], 16)
            for r in range(BT):
                sp.dma_start(wk[:, :, r, :], mixw.rearrange("k o i a -> k o (i a)")).then_inc(s_ld["mixw"], 16)
            sp.dma_start(wn, wmain.rearrange("(c p) h -> p c h", p=P)).then_inc(s_ld["w"], 16)
            sp.dma_start(lbn, lora_b.rearrange("e r h -> (e r) h")).then_inc(s_ld["lora"], 16)
            wait(sp, s_cbias, 16)
            sp.dma_start(bias[0][:, :, :, :].rearrange("p t b c -> p (t b c)"),
                         cbias[0:NT * P].partition_broadcast(P)).then_inc(s_bias[0], 16)

            def step(s, par, k):
                if has(s, 0) and has(s, 2):
                    wait(sp, s_x1, s * NT + NT)
                    sp.dma_start(xs[par][:, :, :],
                                 x_v[bass.ds(s + 2, 1)].rearrange("s p t h -> p (s t) h")).then_inc(s_x[par], 16)
                if has(s, 0) and has(s, 1):
                    wait(sp, s_o1, s * NT)
                    sp.dma_start(bias[1 - par][:, :, :, :].rearrange("p t b c -> p (t b c)"),
                                 cbias[bass.ds((s + 1) * (NT * P), NT * P)].partition_broadcast(P))\
                      .then_inc(s_bias[1 - par], 16)
            supertiles(sp, step)

            with sp.Fori(0, NS) as s:
                for t in range(NT):
                    sp.wait_ge(s_yo[t], s + 1)
                    sp.dma_start(out_v[bass.ds(s * NT + t, 1)].rearrange("n p h -> p (n h)"), yo[t])\
                      .then_inc(s_out[t], 16)
            for t in range(NT):
                sp.wait_ge(s_out[t], 16 * NS)

        @block.gpsimd
        def _(pool):
            pool.memset(ident[:, :], 0.0).then_inc(s_id, 1)
            pool.memset(ones[:, :], 1.0).then_inc(s_id, 1)
            pool.memset(repmask[:, :], 1.0).then_inc(s_id, 1)
            pool.memset(gq, 1.0).then_inc(s_id, 1)
            pool.memset(upper[:, :, :], 1.0).then_inc(s_id, 1)
            pool.wait_ge(s_id, 5)
            pool.affine_select(out=ident[:, :], in_=ident[:, :], compare_op=ALU.not_equal, fill=1.0, base=0,
                               pattern=[[-1, P]], channel_multiplier=1).then_inc(s_const, 1)
            pool.affine_select(out=repmask[:, :], in_=repmask[:, :], compare_op=ALU.is_ge, fill=0.0, base=0,
                               pattern=[[-C, BT]], channel_multiplier=1).then_inc(s_id, 1)
            pool.affine_select(out=gq, in_=gq, compare_op=ALU.is_ge, fill=0.0, base=0,
                               pattern=[[-C, BT], [-CG, C // CG]], channel_multiplier=1).then_inc(s_id, 1)
            pool.wait_ge(s_id, 7)
            pool.affine_select(out=repmask[:, :], in_=repmask[:, :], compare_op=ALU.is_ge, fill=0.0, base=C - 1,
                               pattern=[[C, BT]], channel_multiplier=-1).then_inc(s_const, 1)
            pool.affine_select(out=gq, in_=gq, compare_op=ALU.is_ge, fill=0.0, base=CG - 1,
                               pattern=[[C, BT], [CG, C // CG]], channel_multiplier=-1).then_inc(s_const, 1)
            pool.affine_select(out=upper[:, :, :], in_=upper[:, :, :], compare_op=ALU.is_gt, fill=0.0, base=0,
                               pattern=[[-1, E1], [1, E1]], channel_multiplier=0).then_inc(s_const, 1)
            for e in range(E0):
                pool.memset(sel0[:, e:e + 1], 2.0 - e)
            for c in range(2):
                for e in range(E1):
                    pool.memset(sel1[:, c, e:e + 1], float(c - e))
            pool.memset(mhalf[:, :], -0.5)
            pool.memset(cnt[:, :, :], 0.0).then_inc(s_const, 1)
            pool.memset(cw[:, :, :, :], 0.0).then_inc(s_zero, 1)
            for i in range(2):
                pool.memset(xp[i][:, :, :, 0:1], 0.0)
                pool.memset(xp[i][:, :, :, M + 1:M + 2], 0.0).then_inc(s_zero, 1)
            pool.memset(gw2bd[:, :, :], 0.0).then_inc(s_zero, 1)

            def step(s, par, k):
                if has(s, 2):
                    wait(pool, s_vp, s + 2)
                    if isinstance(s, int) and s == -2:
                        pool.wait_ge(s_msb, C // 4)
                        pool.wait_ge(s_mbsb, 1)
                        pool.wait_ge(s_ss["rs"], 1)
                    pool.tensor_tensor(
                        mixbd[:, :, :, :],
                        mix_all[:, :, bass.ds((s + 2) * (NT * BT), NT * BT)].rearrange("p o (t r) -> p t r o", r=BT),
                        row(row(repmask[:, :], 1, NT), 3, C), ALU.mult).then_inc(s_bd, 1)
                    wait(pool, s_v, s + 2)
                    pool.tensor_tensor(vb[:, :, :], row(mixbias[:, bass.ds((s + 2) * NT, NT)], 2, UC),
                                       row(rs[:, :], 1, NT), ALU.mult).then_inc(s_vb, 1)
                if has(s, 0):
                    for t in range(NT):
                        wait(pool, s_o1h, s * NT + t + 1)
                        pool.tensor_tensor(o1l[t % 2][:, :, :], o1[t % 2][:, :, :, :].rearrange("p q b c -> p q (b c)"),
                                           o1h[t % 2][:, :, :].bitcast(fp32), ALU.subtract).then_inc(s_o1l, 1)
                    wait(pool, s_var, s + 1)
                    pool.tensor_tensor(small[:, 16, :], small[:, 15, :], mhalf[:, :], ALU.pow).then_inc(s_rstd, 1)
            supertiles(pool, step)

            def last_step(s):
                wait(pool, s_w, 1)
                wait(pool, s_ltp, s)
                pool.tensor_tensor(
                    ltw_v,
                    tmp_all[:, bass.ds(s * (NT * ER1), NT * ER1)].rearrange("p (t e r) -> p t e r", t=NT, e=E1),
                    row(wst_all[:, bass.ds(s * NT, NT), 0, :], 3, R1), ALU.mult).then_inc(s_lt, 1)
            last_step(0)
            with pool.Fori(1, NS) as s:
                last_step(s)

        @block.scalar
        def _(act):
            for d in range(2):
                for e in range(E0):
                    act.dma_start(bn[:, :, d, e * R0:(e + 1) * R0],
                                  ffb[e].rearrange("(c p) r -> p c r", p=P)).then_inc(s_ld["bn"], 16)
            for r in range(BT):
                act.dma_start(mbn[:, r, :], mixb).then_inc(s_ld["mixb"], 16)
            act.dma_start(ctxn, ctxw).then_inc(s_ld["ctx"], 16)
            act.dma_start(fsb, fside.partition_broadcast(P)).then_inc(s_ld["ctx"], 16)
            for g in range(C // CG):
                act.dma_start(cwt[g * CG:(g + 1) * CG, :, :],
                              convw[g * CG:(g + 1) * CG].rearrange("o i k -> i o k")).then_inc(s_ld["conv"], 16)
            act.dma_start(gw1n, gw1).then_inc(s_ld["gate"], 16)
            for t in range(NT):
                act.dma_start(gw2n[:, t, :], gw2).then_inc(s_ld["gate"], 16)
            for e in range(E1):
                act.dma_start(ga[:, :, G1 + e * R1:G1 + (e + 1) * R1],
                              lora_a[e].rearrange("(m q) r -> m q r", q=Q)).then_inc(s_ld["gate"], 16)
            for d, src in ((gb1_b, gb1), (gamma_b, gamma), (beta_b, beta), (gb2_b, gb2)):
                act.dma_start(d[:, :], src.partition_broadcast(P)).then_inc(s_ld["rows"], 16)

            act.wait_ge(s_sp["condT"], 1)
            nc.scalar.activation(condT, ps_c[:, 0:P], ACT.Copy).then_inc(s_ss["condT"], 1)
            act.wait_ge(s_sp["h1"], 1)
            act.wait_ge(s_ld["mlp"], 96)
            nc.scalar.activation(h1, ps_t[:, 0:P], ACT.Gelu, bias=b0c).then_inc(s_ss["h1"], 1)
            act.wait_ge(s_sp["h2"], 1)
            nc.scalar.activation(h2, ps_t[:, 0:P], ACT.Gelu, bias=b1c).then_inc(s_ss["h2"], 1)
            act.wait_ge(s_attd, 1)
            nc.scalar.activation(atte, att, ACT.Exp).then_inc(s_atte, 1)
            act.wait_ge(s_ss["ctx"], 1)
            act.dma_start(cbias.rearrange("(b c) -> b c", c=C), ctxb).then_inc(s_cbias, 16)
            for g in range(0, C // 4, 2):
                act.wait_ge(s_mps, g + 1)
                nc.scalar.activation(mix_all[:, 4 * g:4 * g + 4, :].rearrange("p o b -> p (o b)"),
                                     ps_a[0][:, :], ACT.Copy).then_inc(s_msb, 1)
                act.wait_ge(s_mps, g + 2)
                nc.scalar.activation(mix_all[:, 4 * g + 4:4 * g + 8, :].rearrange("p o b -> p (o b)"),
                                     ps_a[1][:, :], ACT.Copy).then_inc(s_msb, 1)

            def step(s, par, k):
                def o_hi(t):
                    act.wait_ge(s_o1, s * NT + t + 1)
                    wait(act, s_mp, s * NT + max(t - 1, 0))
                    nc.scalar.activation(o1h[t % 2][:, :, :], o1[t % 2][:, :, :, :].rearrange("p q b c -> p q (b c)"),
                                         ACT.Copy).then_inc(s_o1h, 1)

                def ga_out(t):
                    act.wait_ge(s_gp, s * NT + t + 1)
                    if t == 0:
                        wait(act, s_h, s)
                    nc.scalar.activation(hs[:, t, :], ps_g[:, 0:G1], ACT.Copy)
                    nc.scalar.activation(tmp_all[:, bass.ds((s * NT + t) * ER1, ER1)], ps_g[:, G1:GC],
                                         ACT.Copy).then_inc(s_g, 1)

                def copies(n, base):
                    for i in range(base, base + n):
                        b, q = i // Q, i % Q
                        last = nc.scalar.activation(
                            xp[1 - par][C * q:C * q + C, b, :, 1:M + 1],
                            y_all[C * b:C * b + C, bass.ds((s + 1) * ST, ST)]
                            .rearrange("p (t q m) -> p t q m", t=NT, q=Q)[:, :, q, :], ACT.Copy)
                    return last

                if has(s, 2):
                    for t in range(NT):
                        act.wait_ge(s_xtp, (s + 2) * NT + t + 1)
                        if t == 0:
                            wait(act, s_up, s + 2)
                        nc.scalar.activation(xT[:, t, :, :].rearrange("p c m -> p (c m)"), ps_a[t % 2][:, :],
                                             ACT.Copy).then_inc(s_xt, 1)
                if has(s, 1):
                    act.wait_ge(s_gtp, s + 2)
                    wait(act, s_dp, (s + 1) * NT)
                    nc.scalar.activation(gmT[:, :], ps_t[:, :], ACT.Copy).then_inc(s_gt, 1)
                if has(s, 0):
                    o_hi(0)
                    ga_out(0)
                if has(s, 1):
                    act.wait_ge(s_x1, (s + 1) * NT + NT)
                    wait(act, s_cp, s * NT)
                    last = copies(3, 8)
                if has(s, 0):
                    o_hi(1)
                    ga_out(1)
                if has(s, 1):
                    last = copies(3, 11)
                if has(s, 0):
                    o_hi(2)
                    ga_out(2)
                if has(s, 1):
                    copies(2, 14).then_inc(s_xpa, 1)
                if has(s, 0):
                    o_hi(3)
                if has(s, 2):
                    act.wait_ge(s_up, s + 3)
                    wait(act, s_vp, s + 2)
                    nc.scalar.activation(u_sb[:, :, :].rearrange("p t c -> p (t c)"), ps_a[0][:, 0:NT * UC],
                                         ACT.Copy).then_inc(s_u, 1)
                if has(s, 0):
                    ga_out(3)
                if has(s, 0):
                    act.wait_ge(s_htp, s + 1)
                    wait(act, s_rp, s)
                    nc.scalar.activation(hT[:, :], ps_t[:, 0:P], ACT.Copy).then_inc(s_ht, 1)
                if has(s, 2):
                    act.wait_ge(s_df0, s + 3)
                    nc.scalar.activation(sc0[:, 1, :, :], sc0[:, 0, :, :], ACT.Exp).then_inc(s_ex0, 1)
                if isinstance(s, int) and s == -2:
                    for q in range(Q):
                        act.wait_ge(s_wps, q + 1)
                        nc.scalar.activation(wt_hi[:, q, :].rearrange("p (q m) -> p q m", q=Q),
                                             ps_d[q % 2][:, :].rearrange("p (m q) -> p q m", q=Q),
                                             ACT.Copy).then_inc(s_whi, 1)
                if has(s, 0):
                    act.wait_ge(s_df1, s + 1)
                    nc.scalar.activation(sc1[:, 2, :, :], sc1[:, 1, :, :], ACT.Exp).then_inc(s_ex1, 1)
            supertiles(act, step)

            def last_step(s):
                act.wait_ge(s_ltp, s + 1)
                wait(act, s_lp, s * NT)
                nc.scalar.activation(lt_hi[:, :], ps_a[0][:, :], ACT.Copy).then_inc(s_lth, 1)
            last_step(0)
            with act.Fori(1, NS) as s:
                last_step(s)

        @block.vector
        def _(dve):
            link, n = chain(dve, s_sd, 0)
            V = nc.vector
            dve.wait_ge(s_ld["conv"], 16 * (C // CG))
            dve.wait_ge(s_const, 3)
            dve.wait_ge(s_zero, 1)
            for r in range(1, BT):
                V.tensor_copy(cwt[C * r:C * r + C, :, :], cwt[0:C, :, :])
            link(V.tensor_reduce(gmask, gq.rearrange("p r g -> p g r"), axis=AXX, op=ALU.add))
            for q in range(Q):
                part = slice(C * q, C * q + C)
                for j in range(SH):
                    ps = [p for p in range(Q) if 0 <= 4 * j + q - p < TAPS]
                    if not ps:
                        continue
                    for p in ps:
                        kk = 4 * j + q - p
                        last = V.tensor_tensor(
                            cw[part, j, p, :].rearrange("i (g o) -> i g o", o=CG),
                            row(cwt[part, :, kk], 1, C // CG), row(gmask[part, :], 2, CG), ALU.mult)
            last.then_inc(s_cw, 1)

            dve.wait_ge(s_sp["pm"], 1)
            V.tensor_copy(pm[:, :, :].rearrange("p c u -> p (c u)"), ps_a[0][:, 0:HC * UC]).then_inc(s_ss["pm"], 1)
            dve.wait_ge(s_sp["ctxT"], 1)
            V.tensor_copy(ctxT, ps_g[:, 0:C]).then_inc(s_ss["ctxT"], 1)
            dve.wait_ge(s_sp["b"], 1)
            qm = "p (m q) -> p q m"
            link(V.tensor_copy(b_hi[:, :].rearrange("p (q m) -> p q m", q=Q), ps_d[0][:, :].rearrange(qm, q=Q)))
            V.tensor_tensor(b_lo[:, :].rearrange("p (q m) -> p q m", q=Q), ps_d[0][:, :].rearrange(qm, q=Q),
                            b_hi[:, :].bitcast(fp32).rearrange("p (q m) -> p q m", q=Q),
                            ALU.subtract).then_inc(s_ss["b"], 1)
            dve.wait_ge(s_sp["gw1"], 1)
            dve.wait_ge(s_zero, 4)
            for t in range(NT):
                V.tensor_copy(gw2bd[G1 * t:G1 * t + G1, t, :], ps_a[1][G1 * t:G1 * t + G1, Q * G1:Q * G1 + E1])
            V.tensor_copy(ga[:, :, 0:G1], ps_a[1][:, 0:Q * G1].rearrange("p (q g) -> p q g", q=Q))\
             .then_inc(s_ss["gw1"], 1)
            dve.wait_ge(s_sp["att"], 1)
            link(V.tensor_tensor(att, ps_t[:, 0:K0], b2b, ALU.add))
            link(V.reduce_max(sm[:, 0:1], att, AXX))
            V.tensor_scalar(att, att, sm[:, 0:1], None, ALU.subtract).then_inc(s_attd, 1)
            dve.wait_ge(s_sp["ctx"], 1)
            dve.wait_ge(s_ld["ctx"], 32)
            V.tensor_tensor(ctxb, ps_g[:, 0:C], fsb, ALU.add).then_inc(s_ss["ctx"], 1)
            dve.wait_ge(s_atte, 1)
            link(V.reduce_sum(sm[:, 1:2], atte, AXX))
            link(V.reciprocal(sm[:, 2:3], sm[:, 1:2]))
            V.tensor_scalar(att, atte, sm[:, 2:3], None, ALU.mult).then_inc(s_ss["att"], 1)
            dve.wait_ge(s_sp["rs"], 1)
            V.tensor_copy(rs[:, :], ps_c[:, 0:UC]).then_inc(s_ss["rs"], 1)
            dve.wait_ge(s_sp["attT"], 1)
            V.tensor_copy(attT, ps_v[0:K0, 0:P]).then_inc(s_ss["attT"], 1)
            dve.wait_ge(s_mbps, 1)
            for r in range(BT):
                last = V.tensor_copy(mixbias[C * r:C * r + C, :],
                                     ps_v[C * r:C * r + C, 128:128 + NB].rearrange("p (n r) -> p n r", r=BT)[:, :, r])
            last.then_inc(s_mbsb, 1)
            dve.wait_ge(s_ld["lora"], 16)
            link(V.tensor_copy(lb_hi[:, :].rearrange("p (q m) -> p q m", q=Q), lbn.rearrange(qm, q=Q)))
            V.tensor_tensor(lb_lo[:, :].rearrange("p (q m) -> p q m", q=Q), lbn.rearrange(qm, q=Q),
                            lb_hi[:, :].bitcast(fp32).rearrange("p (q m) -> p q m", q=Q),
                            ALU.subtract).then_inc(s_lb, 1)
            dve.wait_ge(s_const, 5)
            dve.wait_ge(s_ld["rows"], 16 * 4)

            def step(s, par, k):
                def o_out(t):
                    dve.wait_ge(s_cp, s * NT + t + 1)
                    wait(dve, s_gp, s * NT + max(t - 1, 0))
                    wait(dve, s_o1l, s * NT + max(t - 1, 0))
                    if t == 0:
                        dve.wait_ge(s_bias[par], 16 * (k + 1))
                    V.tensor_tensor(o1[t % 2][:, :, :, :].rearrange("m p b o -> m b p o"),
                                    ps_c[:, :].rearrange("m (b p o) -> m b p o", b=BT, p=Q),
                                    row(bias[par][:, t, :, :], 2, Q), ALU.add).then_inc(s_o1, 1)

                def y_out(t):
                    dve.wait_ge(s_mp, s * NT + t + 1)
                    yt = y_all[:, bass.ds(s * ST + t * H, H)]
                    V.tensor_tensor(yt, ps_d[t % 2][:, :], yt, ALU.add).then_inc(s_y, 1)

                def x1_out(t):
                    dve.wait_ge(s_dp, (s + 1) * NT + t + 1)
                    V.tensor_tensor(y_all[:, bass.ds((s + 1) * ST + t * H, H)].rearrange("p (q m) -> p q m", q=Q),
                                    ps_d[t % 2][:, :].rearrange("p (q m) -> p q m", q=Q),
                                    xs[1 - par][:, t, :].rearrange("p (m q) -> p q m", q=Q), ALU.add)\
                     .then_inc(s_x1, 1)

                def copies(n, base):
                    for i in range(base, base + n):
                        b, q = i // Q, i % Q
                        last = V.tensor_scalar(
                            xp[1 - par][C * q:C * q + C, b, :, 1:M + 1],
                            y_all[C * b:C * b + C, bass.ds((s + 1) * ST, ST)]
                            .rearrange("p (t q m) -> p t q m", t=NT, q=Q)[:, :, q, :], 1.0, None, ALU.mult)
                    return last

                if has(s, 0):
                    o_out(0)
                if has(s, 1):
                    for t in range(NT):
                        x1_out(t)
                    dve.wait_ge(s_x1, (s + 1) * NT + NT)
                    wait(dve, s_cp, s * NT)
                    copies(2, 0)
                if has(s, 0):
                    o_out(1)
                if has(s, 1):
                    copies(3, 2)
                if has(s, 0):
                    y_out(0)
                    o_out(2)
                if has(s, 1):
                    copies(3, 5).then_inc(s_xpd, 1)
                if has(s, 0):
                    y_out(1)
                    o_out(3)
                    y_out(2)
                    link, n = chain(dve, s_c1, s * N_C1)
                    dve.wait_ge(s_g, s * NT + NT)
                    link(V.tensor_tensor(ha[:, :, :], hs[:, :, :], row(gb1_b[:, :], 1, NT), ALU.add))
                    link(V.reduce_sum(small[:, 12, :], ha[:, :, :], AXX))
                    link(V.tensor_scalar(small[:, 13, :], small[:, 12, :], 1.0 / G1, None, ALU.mult))
                    link(V.tensor_tensor(hb[:, :, :], ha[:, :, :], row(small[:, 13, :], 2, G1), ALU.subtract))
                    link(V.tensor_tensor(ha[:, :, :], hb[:, :, :], hb[:, :, :], ALU.mult))
                    link(V.reduce_sum(small[:, 14, :], ha[:, :, :], AXX))
                    V.tensor_scalar(small[:, 15, :], small[:, 14, :], 1.0 / G1, EPS, ALU.mult, ALU.add)\
                     .then_inc(s_var, 1)
                    y_out(3)
                    dve.wait_ge(s_rstd, s + 1)
                    link(V.tensor_tensor(ha[:, :, :], hb[:, :, :], row(small[:, 16, :], 2, G1), ALU.mult))
                    link(V.tensor_tensor(hb[:, :, :], ha[:, :, :], row(gamma_b[:, :], 1, NT), ALU.mult))
                    link(V.tensor_tensor(ha[:, :, :], hb[:, :, :], row(beta_b[:, :], 1, NT), ALU.add))
                    wait(dve, s_htp, s)
                    V.tensor_scalar(hr[:, :, :], ha[:, :, :], 0.0, None, ALU.max).then_inc(s_h, 1)
                    assert n[0] == N_C1, n[0]
                if has(s, 2):
                    link, n = chain(dve, s_c0, (s + 2) * N_C0)
                    dve.wait_ge(s_vp, s + 3)
                    dve.wait_ge(s_vb, s + 3)
                    V.tensor_tensor(v[:, :, :], ps_v[:, 0:NT * UC].rearrange("p (t c) -> p t c", t=NT), vb[:, :, :],
                                    ALU.add).then_inc(s_v, 1)
                    dve.wait_ge(s_v, s + 3)
                    lg = v[:, :, ER0:UC]
                    link(V.reduce_max(small[:, 0, :], lg, AXX))
                    V.tensor_tensor(sc0[:, 0, :, :], lg, row(small[:, 0, :], 2, E0), ALU.subtract).then_inc(s_df0, 1)
                    link(V.tensor_tensor(pair0[:, 0], row(lg, 2, E0), row(lg, 3, E0), ALU.is_gt))
                    link(V.tensor_tensor(pair0[:, 1], pair0[:, 0], row(upper[:, 0:E0, 0:E0], 1, NT), ALU.mult))
                    link(V.reduce_sum(sc0[:, 2], pair0[:, 1], AXX))
                    link(V.reduce_sum(sc0[:, 3], pair0[:, 1].rearrange("p t e j -> p t j e"), AXX))
                    link(V.tensor_tensor(sc0[:, 4], sc0[:, 2], sc0[:, 3], ALU.subtract))
                    link(V.tensor_tensor(sc0[:, 5], sc0[:, 4], row(sel0[:, :], 1, NT), ALU.is_lt))
                    dve.wait_ge(s_ex0, s + 3)
                    link(V.tensor_tensor(sc0[:, 6], sc0[:, 1], sc0[:, 5], ALU.mult))
                    link(V.reduce_sum(small[:, 1, :], sc0[:, 6], AXX))
                    link(V.reciprocal(small[:, 2, :], small[:, 1, :]))
                    link(V.scalar_tensor_tensor(out=sc0[:, 7], in0=sc0[:, 6], scalar=SCALE0,
                                                in1=row(small[:, 2, :], 2, E0), op0=ALU.mult, op1=ALU.mult))
                    link(V.tensor_tensor(gm[:, :, :].rearrange("p t (e r) -> p t e r", e=E0),
                                         v[:, :, 0:ER0].rearrange("p t (e r) -> p t e r", e=E0),
                                         row(sc0[:, 7], 3, R0), ALU.mult))
                    wait(dve, s_gtp, s + 2)
                    link(V.tensor_copy(gms[:, :, 0, :].bitcast(fp32r), gm[:, :, :]))
                    V.tensor_tensor(gms[:, :, 1, :], gm[:, :, :], gms[:, :, 0, :], ALU.subtract).then_inc(s_gm, 1)
                    assert n[0] == N_C0, n[0]
                if isinstance(s, int) and s == -2:
                    for q in range(Q):
                        dve.wait_ge(s_whi, q + 1)
                        V.tensor_tensor(wt_lo[:, q, :].rearrange("p (q m) -> p q m", q=Q),
                                        ps_d[q % 2][:, :].rearrange("p (m q) -> p q m", q=Q),
                                        wt_hi[:, q, :].bitcast(fp32).rearrange("p (q m) -> p q m", q=Q),
                                        ALU.subtract).then_inc(s_wlo, 1)
                if has(s, 0):
                    link, n = chain(dve, s_c2, s * N_C2)
                    dve.wait_ge(s_rp, s + 1)
                    V.tensor_tensor(sc1[:, 0], ps_v[:, 0:NT * E1].rearrange("p (t e) -> p t e", t=NT),
                                    row(gb2_b[:, :], 1, NT), ALU.add).then_inc(s_r, 1)
                    dve.wait_ge(s_r, s + 1)
                    link(V.reduce_max(small[:, 4, :], sc1[:, 0], AXX))
                    V.tensor_tensor(sc1[:, 1], sc1[:, 0], row(small[:, 4, :], 2, E1), ALU.subtract).then_inc(s_df1, 1)
                    link(V.tensor_tensor(pair1[:, 0], row(sc1[:, 0], 2, E1), row(sc1[:, 0], 3, E1), ALU.is_gt))
                    link(V.tensor_tensor(pair1[:, 1], pair1[:, 0], row(upper[:, :, :], 1, NT), ALU.mult))
                    link(V.reduce_sum(sc1[:, 3], pair1[:, 1], AXX))
                    link(V.reduce_sum(sc1[:, 4], pair1[:, 1].rearrange("p t e j -> p t j e"), AXX))
                    link(V.tensor_tensor(sc1[:, 5], sc1[:, 3], sc1[:, 4], ALU.subtract))
                    link(V.tensor_tensor(oh[:, :, :, :], row(sc1[:, 5], 2, 2), row(sel1[:, :, :], 1, NT),
                                         ALU.is_equal))
                    link(V.reduce_sum(cnt1[:, :, :], oh[:, :, :, :].rearrange("p t c e -> p c e t"), AXX))
                    link(V.tensor_tensor(cnt[:, :, :], cnt[:, :, :], cnt1[:, :, :], ALU.add))
                    dve.wait_ge(s_ex1, s + 1)
                    link(V.tensor_tensor(exs1[:, :, :, :], row(sc1[:, 2], 2, 2), oh[:, :, :, :], ALU.mult))
                    exf = exs1[:, :, :, :].rearrange("p t c e -> p t (c e)")
                    link(V.reduce_sum(small[:, 5, :], exf, AXX))
                    link(V.reciprocal(small[:, 6, :], small[:, 5, :]))
                    link(V.tensor_scalar(small[:, 7, :], small[:, 6, :], ALPHA, None, ALU.mult))
                    link(V.tensor_tensor(
                        wst_all[:, bass.ds(s * NT, NT), :, :].rearrange("p t c e -> p t (c e)"), exf,
                        row(small[:, 7, :], 2, 2 * E1), ALU.mult))
                    assert n[0] == N_C2, n[0]
            supertiles(dve, step)

            V.tensor_copy(cnt1[:, :, :], cnt[:, :, :]).then_inc(s_cnt, 1)
            link, n = chain(dve, s_c3, 0)
            dve.wait_ge(s_cntp, 1)
            link(V.tensor_scalar(allowed[:, :, :], ps_v[:, 0:2 * E1].rearrange("p (c e) -> p c e", c=2),
                                 float(CAPACITY), None, ALU.is_le))
            link(V.tensor_tensor(wst_all[:, :, :, :], wst_all[:, :, :, :], row(allowed[:, :, :], 1, NS * NT),
                                 ALU.mult))
            V.tensor_tensor(wst_all[:, :, 0, :], wst_all[:, :, 0, :], wst_all[:, :, 1, :], ALU.add).then_inc(s_w, 1)

            dve.wait_ge(s_y, NS * NT)
            def last_step(s):
                dve.wait_ge(s_lth, s + 1)
                V.tensor_tensor(lt_lo[:, :], ps_a[0][:, :], lt_hi[:, :].bitcast(fp32), ALU.subtract)\
                 .then_inc(s_ltl, 1)
                for t in range(NT):
                    dve.wait_ge(s_lp, s * NT + t + 1)
                    wait(dve, s_out[t], s * 16)
                    V.tensor_tensor(yo[t].rearrange("p (m q) -> p q m", q=Q),
                                    ps_l[t][:, :].rearrange("p (q m) -> p q m", q=Q),
                                    y_all[:, bass.ds(s * ST + t * H, H)].rearrange("p (q m) -> p q m", q=Q),
                                    ALU.add).then_inc(s_yo[t], 1)
            last_step(0)
            with dve.Fori(1, NS) as s:
                last_step(s)

        @block.tensor
        def _(pe):
            T = nc.tensor
            idp = ident[:, :]
            pe.wait_ge(s_const, 1)
            pe.wait_ge(s_ld["cond"], 16)
            T.transpose(ps_c[:, 0:P], condn, idp).then_inc(s_sp["condT"], 1)
            pe.wait_ge(s_ld["aw"], 32)
            for c in range(HC):
                last = T.transpose(ps_a[0][:, c * UC:(c + 1) * UC], aw[:, c * P:(c + 1) * P], ident[0:UC, 0:UC])
            last.then_inc(s_sp["pm"], 1)
            pe.wait_ge(s_ld["mlp"], 96)
            pe.wait_ge(s_ss["condT"], 1)
            T.matmul(ps_t[:, 0:P], w0n, condT, start=True, stop=True).then_inc(s_sp["h1"], 1)
            pe.wait_ge(s_ld["ctx"], 32)
            T.transpose(ps_g[:, 0:C], ctxn, ident[0:C, 0:C]).then_inc(s_sp["ctxT"], 1)
            pe.wait_ge(s_ss["h1"], 1)
            T.matmul(ps_t[:, 0:P], w1n, h1, start=True, stop=True).then_inc(s_sp["h2"], 1)
            pe.wait_ge(s_ld["bn"], 16 * 2 * E0)
            for c in range(HC):
                last = T.transpose(ps_d[0][:, c * P:(c + 1) * P], bn[:, c, :, :].rearrange("p d e -> p (d e)"), idp)
            last.then_inc(s_sp["b"], 1)
            pe.wait_ge(s_ss["h2"], 1)
            T.matmul(ps_t[:, 0:K0], h2, w2n, start=True, stop=True).then_inc(s_sp["att"], 1)
            pe.wait_ge(s_ld["gate"], 16 * (1 + NT + E1))
            for q in range(Q):
                last = T.transpose(ps_a[1][:, q * G1:(q + 1) * G1],
                                   gw1n.rearrange("p (m q) -> p q m", q=Q)[:, q, :], ident[0:G1, 0:G1])
            T.transpose(ps_a[1][:, Q * G1:Q * G1 + E1], gw2n.rearrange("e t c -> e (t c)"), ident[0:E1, 0:E1])\
             .then_inc(s_sp["gw1"], 1)
            pe.wait_ge(s_ss["ctxT"], 1)
            T.matmul(ps_g[:, 0:C], condT, ctxT, start=True, stop=True).then_inc(s_sp["ctx"], 1)
            pe.wait_ge(s_ss["pm"], 1)
            for c in range(HC):
                last = T.matmul(ps_c[:, 0:UC], ones[:, :], pm[:, c, :], start=(c == 0), stop=(c == HC - 1))
            last.then_inc(s_sp["rs"], 1)
            pe.wait_ge(s_ss["att"], 1)
            T.transpose(ps_v[0:K0, 0:P], att, idp).then_inc(s_sp["attT"], 1)
            pe.wait_ge(s_ss["attT"], 1)
            pe.wait_ge(s_ld["mixw"], 16 * BT)
            pe.wait_ge(s_ld["mixb"], 16 * BT)
            pe.wait_ge(s_ss["gw1"], 1)
            T.matmul(ps_v[:, P:P + NB], mbn.rearrange("k r o -> k (r o)"), attT, start=True, stop=True)\
             .then_inc(s_mbps, 1)
            for g in range(C // 4):
                if g >= 2:
                    pe.wait_ge(s_msb, g - 1)
                for o in range(4):
                    last = T.matmul(ps_a[g % 2][:, o * NB:(o + 1) * NB],
                                    wk[:, 4 * g + o, :, :].rearrange("k r i -> k (r i)"), attT,
                                    start=True, stop=True)
                last.then_inc(s_mps, 1)
            pe.wait_ge(s_msb, C // 4)
            pe.wait_ge(s_mbsb, 1)
            pe.wait_ge(s_cw, 1)
            pe.wait_ge(s_zero, 4)

            def step(s, par, k):
                def conv(t):
                    if t == 0:
                        pe.wait_ge(s_xpd, s + 1)
                        pe.wait_ge(s_xpa, s + 1)
                    wait(pe, s_o1, s * NT + t)
                    for b in range(BT):
                        for j in range(SH):
                            last = T.matmul(ps_c[:, b * P:(b + 1) * P], xp[par][:, b, t, j:j + M],
                                            cw[:, j, :, :].rearrange("p q o -> p (q o)"),
                                            start=(j == 0), stop=(j == SH - 1))
                    last.then_inc(s_cp, 1)

                def gates(t):
                    pe.wait_ge(s_o1, s * NT + t + 1)
                    wait(pe, s_g, s * NT + t)
                    for q in range(Q):
                        last = T.matmul(ps_g[:, 0:GC], o1[t % 2][:, q, :, :].rearrange("p b c -> p (b c)"),
                                        ga[:, q, :], start=(q == 0), stop=(q == Q - 1))
                    last.then_inc(s_gp, 1)

                def main(t):
                    pe.wait_ge(s_o1l, s * NT + t + 1)
                    if t < 2 and has(s, 1):
                        pe.wait_ge(s_x1, (s + 1) * NT + 3 + t)
                    else:
                        wait(pe, s_y, s * NT + t - 1)
                    n = 0
                    for q in range(Q):
                        for a, w in ((o1h, wt_hi), (o1h, wt_lo), (o1l, wt_hi)):
                            last = T.matmul(ps_d[t % 2][:, :], a[t % 2][:, q, :], w[:, q, :],
                                            start=(n == 0), stop=(n == 3 * Q - 1))
                            n += 1
                    last.then_inc(s_mp, 1)

                if has(s, 2):
                    pe.wait_ge(s_x[par], 16 * (k + 2))
                    for t in range(NT):
                        if t == 0:
                            wait(pe, s_u, s + 2)
                        wait(pe, s_xt, (s + 2) * NT + max(t - 1, 0))
                        for c in range(HC):
                            last = T.transpose(ps_a[t % 2][:, c * P:(c + 1) * P],
                                               xs[par][:, t, c * P:(c + 1) * P], idp)
                        last.then_inc(s_xtp, 1)
                if has(s, 0):
                    conv(0)
                if has(s, 1):
                    pe.wait_ge(s_gm, s + 2)
                    wait(pe, s_ht, s)
                    for t in range(NT):
                        last = T.transpose(ps_t[:, t * P:(t + 1) * P],
                                           gms[:, t, :, :].rearrange("p a c -> p (a c)"), idp)
                    last.then_inc(s_gtp, 1)
                if has(s, 0):
                    gates(0)
                if has(s, 1):
                    pe.wait_ge(s_gt, s + 2)
                    for t in range(NT):
                        if t < 2:
                            wait(pe, s_y, s * NT)
                            wait(pe, s_x1, s * NT + NT)
                            if isinstance(s, int) and s == -1:
                                pe.wait_ge(s_wlo, Q)
                        else:
                            pe.wait_ge(s_x1, (s + 1) * NT + t - 1)
                        lhs = gmT[:, t * P:(t + 1) * P]
                        T.matmul(ps_d[t % 2][:, :], lhs, b_hi[:, :], start=True, stop=False)
                        T.matmul(ps_d[t % 2][:, :], lhs, b_lo[:, :], start=False, stop=True).then_inc(s_dp, 1)
                if has(s, 0):
                    conv(1)
                    main(0)
                    gates(1)
                    conv(2)
                    main(1)
                    gates(2)
                    conv(3)
                    main(2)
                if has(s, 2):
                    pe.wait_ge(s_xt, (s + 2) * NT + NT)
                    for t in range(NT):
                        for c in range(HC):
                            last = T.matmul(ps_a[0][:, t * UC:(t + 1) * UC], xT[:, t, c, :], pm[:, c, :],
                                            start=(c == 0), stop=(c == HC - 1))
                    last.then_inc(s_up, 1)
                if has(s, 0):
                    gates(3)
                    main(3)
                if has(s, 2):
                    pe.wait_ge(s_u, s + 3)
                    pe.wait_ge(s_bd, s + 3)
                    wait(pe, s_v, s + 2)
                    wait(pe, s_r, s)
                    for t in range(NT):
                        last = T.matmul(ps_v[:, t * UC:(t + 1) * UC],
                                        mixbd[:, t, :, :].rearrange("p r o -> p (r o)"), u_sb[:, t, :],
                                        start=True, stop=True)
                    last.then_inc(s_vp, 1)
                if isinstance(s, int) and s == -2:
                    pe.wait_ge(s_ld["w"], 16)
                    for q in range(Q):
                        pe.wait_ge(s_ss["b"], 1) if q < 2 else pe.wait_ge(s_wlo, q - 1)
                        for c in range(HC):
                            last = T.transpose(ps_d[q % 2][:, c * P:(c + 1) * P],
                                               wn[:, c, :].rearrange("p (m q) -> p q m", q=Q)[:, q, :], idp)
                        last.then_inc(s_wps, 1)
                if has(s, 0):
                    pe.wait_ge(s_h, s + 1)
                    pe.wait_ge(s_gt, min(s + 2, NS) if isinstance(s, int) else s + 2)
                    T.transpose(ps_t[:, 0:P], hr[:, :, :].rearrange("p t g -> p (t g)"), idp).then_inc(s_htp, 1)
                    pe.wait_ge(s_ht, s + 1)
                    pe.wait_ge(s_v, min(s + 3, NS) if isinstance(s, int) else s + 3)
                    T.matmul(ps_v[:, 0:NT * E1], hT[:, :], gw2bd[:, :, :].rearrange("p t e -> p (t e)"),
                             start=True, stop=True).then_inc(s_rp, 1)
            supertiles(pe, step)

            pe.wait_ge(s_cnt, 1)
            T.matmul(ps_v[:, 0:2 * E1], ones[:, :], cnt1[:, :, :].rearrange("p c e -> p (c e)"),
                     start=True, stop=True).then_inc(s_cntp, 1)
            pe.wait_ge(s_lb, 1)
            def last_step(s):
                pe.wait_ge(s_lt, s + 1)
                wait(pe, s_ltl, s)
                for t in range(NT):
                    last = T.transpose(ps_a[0][:, t * P:(t + 1) * P], ltw[:, 0, t * P:(t + 1) * P], idp)
                last.then_inc(s_ltp, 1)
                pe.wait_ge(s_ltl, s + 1)
                for t in range(NT):
                    wait(pe, s_yo[t], s)
                    for n, (a, w) in enumerate(((lt_hi, lb_hi), (lt_hi, lb_lo), (lt_lo, lb_hi))):
                        last = T.matmul(ps_l[t][:, :], a[:, t * P:(t + 1) * P], w[:, :],
                                        start=(n == 0), stop=(n == 2))
                    last.then_inc(s_lp, 1)
            last_step(0)
            with pe.Fori(1, NS) as s:
                last_step(s)


_INS = ['x', 'cond_128', 'fside_S_0', 'L0_cond_W0', 'L0_cond_b0', 'L0_cond_W1', 'L0_cond_b1', 'L0_cond_W2',
        'L0_cond_b2', 'L0_cond_weight', 'L0_cond_bias_k', 'L0_ffn_A', 'L0_ffn_B', 'L0_ffn_Wr', 'L1_cond_weight',
        'L1_cond_c_weight', 'L1_ffn_weight', 'L1_ffn_lora_A', 'L1_ffn_lora_B', 'L1_ffn_gw1', 'L1_ffn_gb1',
        'L1_ffn_ln_gamma', 'L1_ffn_ln_beta', 'L1_ffn_gw2', 'L1_ffn_gb2']


def kernel(**inputs):
    import numpy as _np
    import concourse.bacc as _bacc
    from concourse import mybir as _mybir
    from concourse.bass_utils import run_bass_kernel_spmd as _run

    nc = _bacc.Bacc("TRN2", target_bir_lowering=False, num_devices=1)
    arrays, args = {}, []
    for name in _INS:
        a = _np.ascontiguousarray(inputs[name])
        arrays[f"in_{name}_dram"] = a
        args.append(nc.dram_tensor(f"in_{name}_dram", a.shape, _mybir.dt.from_np(a.dtype), kind="ExternalInput").ap())
    shape = _np.shape(inputs['x'])
    args.append(nc.dram_tensor("out_dram", shape, _mybir.dt.float32, kind="ExternalOutput").ap())
    adaln_ffn_kernel(nc, *args)
    r = _run(nc, [arrays], core_ids=[0])
    return r.results[0]["out_dram"]
```

```python
import concourse.bass as bass
from concourse import mybir
from contextlib import ExitStack



def adaln_ffn_kernel(nc: bass.Bass, x, cond, fside, w0, b0, w1, b1, w2, b2, mixw, mixb, ffa, ffb, ffr,
                     convw, ctxw, wmain, lora_a, lora_b, gw1, gb1, gamma, beta, gw2, gb2, out):
    fp32 = mybir.dt.float32
    fp32r = mybir.dt.float32r
    ALU = mybir.AluOpType
    ACT = mybir.ActivationFunctionType
    AXX = mybir.AxisListType.X

    P = 128
    NB, C, H = x.shape
    K0 = mixw.shape[0]
    E0, R0 = ffa.shape[0], ffa.shape[1]
    ER0 = E0 * R0
    UC = ER0 + E0
    SCALE0 = 16.0 / float(R0) ** 0.5
    E1, R1 = lora_a.shape[0], lora_a.shape[2]
    ER1 = E1 * R1
    G1 = gw1.shape[0]
    GC = G1 + ER1
    TAPS = convw.shape[2]
    CG = convw.shape[1]
    CAPACITY = int(3.0 * NB * C / E1)
    ALPHA = 1.0 / R1
    EPS = 1e-05
    BT = P // C
    NT = 4
    NS = NB // (BT * NT)
    Q = 4
    M = H // Q
    HC = H // P
    SH = 3
    ST = NT * H

    x_v = x.rearrange("(s t b) c h -> s (b c) t h", t=NT, b=BT)
    out_v = out.rearrange("(n b) c h -> n (b c) h", b=BT)

    ctx = ExitStack()
    with ctx:
        def sb(name, shape, dt=fp32):
            return ctx.enter_context(nc.sbuf_tensor(name, shape, dt))

        def sem(name):
            return ctx.enter_context(nc.semaphore(name))

        def row(v, axis, n):
            v = v.unsqueeze(axis)
            shape = list(v.shape)
            shape[axis] = n
            return v.broadcast_to(shape)

        def wait(eng, s, value):
            if not isinstance(value, int) or value > 0:
                eng.wait_ge(s, value)

        y_all = sb("y_all", [P, NS * ST])
        tmp_all = sb("tmp_all", [P, NS * NT * ER1])
        wst_all = sb("wst_all", [P, NS * NT, 2, E1])
        mix_all = sb("mix_all", [P, C, NB])
        wt_hi = sb("wt_hi", [P, Q, H], fp32r)
        wt_lo = sb("wt_lo", [P, Q, H], fp32r)
        xs = [sb(f"xs{i}", [P, NT, H]) for i in range(2)]
        xT = sb("xT", [P, NT, HC, P])
        xp = [sb(f"xp{i}", [P, BT, NT, M + 2]) for i in range(2)]
        o1 = [sb(f"o1_{i}", [P, Q, BT, C]) for i in range(2)]
        o1h = [sb(f"o1h{i}", [P, Q, P], fp32r) for i in range(2)]
        o1l = [sb(f"o1l{i}", [P, Q, P], fp32r) for i in range(2)]
        bias = [sb(f"bias{i}", [P, NT, BT, C]) for i in range(2)]
        mixbd = sb("mixbd", [P, NT, BT, C])
        mixbias = sb("mixbias", [P, NS * NT])
        pm = sb("pm", [P, HC, UC])
        rs = sb("rs", [P, UC])
        b_hi = sb("b_hi", [P, H], fp32r)
        b_lo = sb("b_lo", [P, H], fp32r)
        ga = sb("ga", [P, Q, GC])
        cw = sb("cw", [P, SH, Q, C])
        lb_hi = sb("lb_hi", [P, H], fp32r)
        lb_lo = sb("lb_lo", [P, H], fp32r)
        gw2bd = sb("gw2bd", [P, NT, E1])
        ident = sb("ident", [P, P])
        ones = sb("ones", [P, P])
        u_sb = sb("u_sb", [P, NT, UC])
        vb = sb("vb", [P, NT, UC])
        v = sb("v", [P, NT, UC])
        gms = sb("gms", [P, NT, 2, ER0])
        gm = sb("gm", [P, NT, ER0])
        gmT = sb("gmT", [P, NT * P], fp32r)
        hs = sb("hs", [P, NT, G1])
        ha = sb("ha", [P, NT, G1])
        hb = sb("hb", [P, NT, G1])
        hr = sb("hr", [P, NT, G1])
        hT = sb("hT", [P, P])
        gb1_b = sb("gb1_b", [P, G1])
        gamma_b = sb("gamma_b", [P, G1])
        beta_b = sb("beta_b", [P, G1])
        gb2_b = sb("gb2_b", [P, E1])
        repmask = sb("repmask", [P, BT])
        upper = sb("upper", [P, E1, E1])
        sel0 = sb("sel0", [P, E0])
        sel1 = sb("sel1", [P, 2, E1])
        mhalf = sb("mhalf", [P, NT])
        small = sb("small", [P, 24, NT])
        sc0 = sb("sc0", [P, 8, NT, E0])
        pair0 = sb("pair0", [P, 2, NT, E0, E0])
        sc1 = sb("sc1", [P, 6, NT, E1])
        oh = sb("oh", [P, NT, 2, E1])
        exs1 = sb("exs1", [P, NT, 2, E1])
        pair1 = sb("pair1", [P, 2, NT, E1, E1])
        cnt = sb("cnt", [P, 2, E1])
        cnt1 = sb("cnt1", [P, 2, E1])
        allowed = sb("allowed", [P, 2, E1])

        at = [2 * ST]

        def early(parts, shape):
            n = 1
            for d in shape:
                n *= d
            a = y_all[0:parts, at[0]:at[0] + n]
            at[0] += n
            assert at[0] <= NS * ST
            if len(shape) == 1:
                return a
            names = "abcd"[:len(shape)]
            return a.rearrange(f"p ({' '.join(names)}) -> p {' '.join(names)}",
                               **{k: d for k, d in zip(names[1:], shape[1:])})

        wn = early(P, [HC, H])
        wk = early(K0, [C, C])
        mixn = early(P, [C, BT, C])
        bn = early(P, [HC, ER0])
        bn2 = early(P, [HC, 2, ER0])
        aw = early(UC, [H])
        gw1n = early(G1, [H])
        gw2n = early(E1, [NT, G1])
        lbn = early(P, [H])
        condn = early(P, [P])
        w0n = early(P, [P])
        w1n = early(P, [P])
        condT = early(P, [P])
        h1 = early(P, [P])
        h2 = early(P, [P])
        w2n = early(P, [K0])
        b0c = early(P, [1])
        b1c = early(P, [1])
        b2b = early(P, [K0])
        mbn = early(K0, [BT, C])
        ctxn = early(C, [P])
        ctxT = early(P, [C])
        ctxb = early(P, [C])
        fsb = early(P, [C])
        cwt = early(P, [CG, TAPS])
        att = early(P, [K0])
        atte = early(P, [K0])
        attT = early(K0, [P])
        gq = early(P, [BT, C // CG])
        gmask = early(P, [C // CG])
        sm = early(P, [4])

        def pb(name):
            return ctx.enter_context(nc.psum_tensor(name, [P, 512], fp32))

        ps_a = [pb("ps_a0"), pb("ps_a1")]
        ps_t = pb("ps_t")
        ps_v = pb("ps_v")
        ps_d = [pb("ps_d0"), pb("ps_d1")]
        ps_c = pb("ps_c")
        ps_g = pb("ps_g")

        cbias = nc.dram_tensor("cbias", (NB * C,), fp32).ap()

        s_x = [sem(f"x_loaded{i}") for i in range(2)]
        s_bias = [sem(f"bias_loaded{i}") for i in range(2)]
        s_ld = {n: sem(f"ld_{n}") for n in ("cond", "mlp", "aw", "mixw", "mixb", "bn", "w", "gate", "ctx", "conv",
                                            "lora", "lora_a", "rows")}
        s_cbias = sem("cbias_stored")
        s_id = sem("ident_steps")
        s_const = sem("consts_ready")
        s_zero = sem("zeros_ready")
        names = ("condT", "pm", "h1", "ctxT", "b", "h2", "gw1", "att", "ctx", "rs", "attT", "mix0", "mix1")
        s_sp = {n: sem(f"setup_ps_{n}") for n in names}
        s_ss = {n: sem(f"setup_sb_{n}") for n in names}
        s_wps, s_whi, s_wlo = sem("w_ps"), sem("w_hi"), sem("w_lo")
        s_mps, s_msa, s_msd = sem("mix_ps"), sem("mix_copied_act"), sem("mix_copied_dve")
        s_mbps, s_mbsb = sem("mixbias_ps"), sem("mixbias_sb")
        s_cw, s_bn = sem("convw_ready"), sem("b_doubled")
        s_lb = sem("lora_b_split")
        s_sc, s_sd = sem("setup_chain_act"), sem("setup_chain_dve")
        s_attd, s_atte = sem("att_shifted"), sem("att_exp")

        s_xtp, s_xt = sem("xT_ps"), sem("xT_copied")
        s_up, s_u = sem("u_ps"), sem("u_copied")
        s_bd, s_vb = sem("mixbd_ready"), sem("vbias_ready")
        s_vp, s_v = sem("v_ps"), sem("v_ready")
        s_df0, s_ex0 = sem("gate0_shifted"), sem("gate0_exp")
        s_c0 = sem("gate0_chain")
        s_gm, s_gtp, s_gt = sem("gm_ready"), sem("gmT_ps"), sem("gmT_copied")
        s_dp, s_x1 = sem("delta_ps"), sem("x1_ready")
        s_xpd, s_xpa = sem("xp_dve"), sem("xp_act")
        s_cp, s_o1 = sem("conv_ps"), sem("o1_ready")
        s_o1h, s_o1l = sem("o1_hi"), sem("o1_lo")
        s_gp, s_g = sem("ga_ps"), sem("ga_copied")
        s_mp, s_y = sem("main_ps"), sem("y_ready")
        s_c1 = sem("norm_chain")
        s_var, s_rstd = sem("var_ready"), sem("rstd_ready")
        s_h, s_htp, s_ht = sem("hidden_ready"), sem("hT_ps"), sem("hT_copied")
        s_rp, s_r = sem("router_ps"), sem("router_read")
        s_df1, s_ex1 = sem("gate1_shifted"), sem("gate1_exp")
        s_c2 = sem("gate1_chain")
        s_cnt, s_cntp, s_w = sem("counts_ready"), sem("counts_ps"), sem("weights_ready")
        s_c3 = sem("allowed_chain")
        s_lt, s_ltp = sem("weighted"), sem("weighted_ps")
        s_lth, s_ltl = sem("weightedT_hi"), sem("weightedT_lo")
        s_lp, s_yo = sem("lora_ps"), [sem(f"out_ready{i}") for i in range(NT)]
        s_out = [sem(f"out_stored{i}") for i in range(NT)]

        ltw = [xs[0][:, i, :] for i in range(2)]
        lt_hi = [wt_hi[:, i, :] for i in range(2)]
        lt_lo = [wt_lo[:, i, :] for i in range(2)]
        yo = [xT[:, t, :, :].rearrange("p c m -> p (c m)") for t in range(NT)]
        ps_l = [ps_d[0], ps_d[1], ps_c, ps_g]

        MG = C // 4
        ps_m = [ps_c, ps_g, ps_d[0], ps_d[1]]

        def chain(eng, s, base):
            n = [0]

            def link(ins):
                n[0] += 1
                ins.then_inc(s, 1)
                eng.wait_ge(s, base + n[0])
            return link, n

        N_C0, N_C1, N_C2 = 13, 9, 14

        def steps(eng, step, first, last):
            for s in range(first, 2):
                step(s, s % 2, s // 2)
            with eng.Fori(1, NS // 2 - 1) as k:
                step(k * 2, 0, k)
                step(k * 2 + 1, 1, k)
            for s in range(NS - 2, last + 1):
                step(s, s % 2, s // 2)

        def has(s, ahead):
            return not isinstance(s, int) or 0 <= s + ahead < NS

        def upto(count, most):
            return min(count, most) if isinstance(count, int) else count

        block = ctx.enter_context(nc.Block())

        @block.sync
        def _(sp):
            sp.dma_start(condn, cond).then_inc(s_ld["cond"], 16)
            sp.dma_start(w0n, w0).then_inc(s_ld["mlp"], 16)
            sp.dma_start(xs[0][:, :, :], x_v[0]).then_inc(s_x[0], 16)
            sp.dma_start(w1n, w1).then_inc(s_ld["mlp"], 16)
            sp.dma_start(w2n, w2).then_inc(s_ld["mlp"], 16)
            sp.dma_start(ctxn, ctxw).then_inc(s_ld["ctx"], 16)
            sp.dma_start(wk, mixw.rearrange("k o i a -> k o (i a)")).then_inc(s_ld["mixw"], 16)
            sp.dma_start(mbn, row(mixb, 1, BT)).then_inc(s_ld["mixb"], 16)
            for e in range(E0):
                sp.dma_start(bn[:, :, e * R0:(e + 1) * R0],
                             ffb[e].rearrange("(c p) r -> p c r", p=P)).then_inc(s_ld["bn"], 16)
            sp.dma_start(gw1n, gw1).then_inc(s_ld["gate"], 16)
            sp.dma_start(gw2n, row(gw2, 1, NT)).then_inc(s_ld["gate"], 16)
            sp.dma_start(wn, wmain.rearrange("(c p) h -> p c h", p=P)).then_inc(s_ld["w"], 16)
            sp.dma_start(xs[1][:, :, :], x_v[1]).then_inc(s_x[1], 16)
            for g in range(C // CG):
                sp.dma_start(cwt[g * CG:(g + 1) * CG, :, :],
                             convw[g * CG:(g + 1) * CG].rearrange("o i k -> i o k")).then_inc(s_ld["conv"], 16)
            for e in range(E1):
                sp.dma_start(ga[:, :, G1 + e * R1:G1 + (e + 1) * R1],
                             lora_a[e].rearrange("(m q) r -> m q r", q=Q)).then_inc(s_ld["lora_a"], 16)
            sp.dma_start(lbn, lora_b.rearrange("e r h -> (e r) h")).then_inc(s_ld["lora"], 16)
            wait(sp, s_cbias, 16)
            sp.dma_start(bias[0][:, :, :, :].rearrange("p t b c -> p (t b c)"),
                         cbias[0:NT * P].partition_broadcast(P)).then_inc(s_bias[0], 16)

            def step(s, par, k):
                if has(s, 0) and has(s, 2):
                    wait(sp, s_x1, s * NT + NT)
                    sp.dma_start(xs[par][:, :, :],
                                 x_v[bass.ds(s + 2, 1)].rearrange("s p t h -> p (s t) h")).then_inc(s_x[par], 16)
                if has(s, 0) and has(s, 1):
                    wait(sp, s_o1, s * NT)
                    sp.dma_start(bias[1 - par][:, :, :, :].rearrange("p t b c -> p (t b c)"),
                                 cbias[bass.ds((s + 1) * (NT * P), NT * P)].partition_broadcast(P))\
                      .then_inc(s_bias[1 - par], 16)
            steps(sp, step, -1, NS - 1)

            with sp.Fori(0, NS) as s:
                for t in range(NT):
                    sp.wait_ge(s_yo[t], s + 1)
                    sp.dma_start(out_v[bass.ds(s * NT + t, 1)].rearrange("n p h -> p (n h)"), yo[t])\
                      .then_inc(s_out[t], 16)
            for t in range(NT):
                sp.wait_ge(s_out[t], 16 * NS)

        @block.gpsimd
        def _(pool):
            pool.memset(ident[:, :], 0.0).then_inc(s_id, 1)
            pool.memset(ones[:, :], 1.0).then_inc(s_id, 1)
            pool.memset(repmask[:, :], 1.0).then_inc(s_id, 1)
            pool.memset(gq, 1.0).then_inc(s_id, 1)
            pool.memset(upper[:, :, :], 1.0).then_inc(s_id, 1)
            pool.wait_ge(s_id, 5)
            pool.affine_select(out=ident[:, :], in_=ident[:, :], compare_op=ALU.not_equal, fill=1.0, base=0,
                               pattern=[[-1, P]], channel_multiplier=1).then_inc(s_const, 1)
            pool.affine_select(out=repmask[:, :], in_=repmask[:, :], compare_op=ALU.is_ge, fill=0.0, base=0,
                               pattern=[[-C, BT]], channel_multiplier=1).then_inc(s_id, 1)
            pool.affine_select(out=gq, in_=gq, compare_op=ALU.is_ge, fill=0.0, base=0,
                               pattern=[[-C, BT], [-CG, C // CG]], channel_multiplier=1).then_inc(s_id, 1)
            pool.wait_ge(s_id, 7)
            pool.affine_select(out=repmask[:, :], in_=repmask[:, :], compare_op=ALU.is_ge, fill=0.0, base=C - 1,
                               pattern=[[C, BT]], channel_multiplier=-1).then_inc(s_const, 1)
            pool.affine_select(out=gq, in_=gq, compare_op=ALU.is_ge, fill=0.0, base=CG - 1,
                               pattern=[[C, BT], [CG, C // CG]], channel_multiplier=-1).then_inc(s_const, 1)
            pool.affine_select(out=upper[:, :, :], in_=upper[:, :, :], compare_op=ALU.is_gt, fill=0.0, base=0,
                               pattern=[[-1, E1], [1, E1]], channel_multiplier=0).then_inc(s_const, 1)
            for e in range(E0):
                pool.memset(sel0[:, e:e + 1], 2.0 - e)
            for c in range(2):
                for e in range(E1):
                    pool.memset(sel1[:, c, e:e + 1], float(c - e))
            pool.memset(mhalf[:, :], -0.5)
            pool.memset(cnt[:, :, :], 0.0).then_inc(s_const, 1)
            pool.memset(cw[:, :, :, :], 0.0).then_inc(s_zero, 1)
            for i in range(2):
                pool.memset(xp[i][:, :, :, 0:1], 0.0)
                pool.memset(xp[i][:, :, :, M + 1:M + 2], 0.0).then_inc(s_zero, 1)
            pool.memset(gw2bd[:, :, :], 0.0).then_inc(s_zero, 1)

            for d, src in ((gb1_b, gb1), (gamma_b, gamma), (beta_b, beta), (gb2_b, gb2)):
                pool.dma_start(d[:, :], src.partition_broadcast(P)).then_inc(s_ld["rows"], 16)

            def mixing(u):
                wait(pool, s_vp, u)
                pool.tensor_tensor(
                    mixbd[:, :, :, :],
                    mix_all[:, :, bass.ds(u * (NT * BT), NT * BT)].rearrange("p o (t r) -> p t r o", r=BT),
                    row(row(repmask[:, :], 1, NT), 3, C), ALU.mult).then_inc(s_bd, 1)
                wait(pool, s_v, u)
                pool.tensor_tensor(vb[:, :, :], row(mixbias[:, bass.ds(u * NT, NT)], 2, UC),
                                   row(rs[:, :], 1, NT), ALU.mult).then_inc(s_vb, 1)

            pool.wait_ge(s_ld["bn"], 16 * E0)
            pool.tensor_copy(bn2, row(bn, 2, 2)).then_inc(s_bn, 1)
            pool.wait_ge(s_const, 5)
            pool.wait_ge(s_msa, MG // 2)
            pool.wait_ge(s_msd, MG // 2)
            pool.wait_ge(s_mbsb, 1)
            pool.wait_ge(s_ss["rs"], 1)
            mixing(0)

            def step(s, par, k):
                if has(s, 2):
                    mixing(s + 2)
                if has(s, 0):
                    for t in range(NT):
                        pool.wait_ge(s_o1h, s * NT + t + 1)
                        pool.tensor_tensor(o1l[t % 2][:, :, :], o1[t % 2][:, :, :, :].rearrange("p q b c -> p q (b c)"),
                                           o1h[t % 2][:, :, :].bitcast(fp32), ALU.subtract).then_inc(s_o1l, 1)
                    pool.wait_ge(s_var, s + 1)
                    pool.tensor_tensor(small[:, 16, :], small[:, 15, :], mhalf[:, :], ALU.pow).then_inc(s_rstd, 1)
            steps(pool, step, -1, NS - 1)

            pool.wait_ge(s_w, 1)

            def weigh(s, par, k):
                if has(s, 1):
                    wait(pool, s_ltp, s)
                    pool.tensor_tensor(
                        ltw[1 - par].rearrange("p (t e r) -> p t e r", t=NT, e=E1),
                        tmp_all[:, bass.ds((s + 1) * (NT * ER1), NT * ER1)]
                        .rearrange("p (t e r) -> p t e r", t=NT, e=E1),
                        row(wst_all[:, bass.ds((s + 1) * NT, NT), 0, :], 3, R1), ALU.mult).then_inc(s_lt, 1)
            steps(pool, weigh, -1, NS - 1)

        @block.scalar
        def _(act):
            act.dma_start(aw[0:ER0], ffa.rearrange("e r h -> (e r) h")).then_inc(s_ld["aw"], 16)
            act.dma_start(aw[ER0:UC], ffr).then_inc(s_ld["aw"], 16)
            act.dma_start(b0c, b0.rearrange("(p a) -> p a", a=1)).then_inc(s_ld["mlp"], 16)
            act.dma_start(b1c, b1.rearrange("(p a) -> p a", a=1)).then_inc(s_ld["mlp"], 16)
            act.dma_start(b2b, b2.partition_broadcast(P)).then_inc(s_ld["mlp"], 16)
            act.dma_start(fsb, fside.partition_broadcast(P)).then_inc(s_ld["ctx"], 16)

            def x_transposed(u):
                for t in range(NT):
                    act.wait_ge(s_xtp, u * NT + t + 1)
                    if t == 0:
                        wait(act, s_up, u)
                    nc.scalar.activation(xT[:, t, :, :].rearrange("p c m -> p (c m)"), ps_a[t % 2][:, :],
                                         ACT.Copy).then_inc(s_xt, 1)

            def u_out(u):
                act.wait_ge(s_up, u + 1)
                wait(act, s_vp, u)
                nc.scalar.activation(u_sb[:, :, :].rearrange("p t c -> p (t c)"), ps_a[0][:, 0:NT * UC],
                                     ACT.Copy).then_inc(s_u, 1)

            def gate0_exp(u):
                act.wait_ge(s_df0, u + 1)
                nc.scalar.activation(sc0[:, 1, :, :], sc0[:, 0, :, :], ACT.Exp).then_inc(s_ex0, 1)

            act.wait_ge(s_sp["condT"], 1)
            nc.scalar.activation(condT, ps_c[:, 0:P], ACT.Copy).then_inc(s_ss["condT"], 1)
            act.wait_ge(s_sp["h1"], 1)
            act.wait_ge(s_ld["mlp"], 96)
            nc.scalar.activation(h1, ps_t[:, 0:P], ACT.Gelu, bias=b0c).then_inc(s_ss["h1"], 1)
            act.wait_ge(s_sp["h2"], 1)
            nc.scalar.activation(h2, ps_t[:, 0:P], ACT.Gelu, bias=b1c).then_inc(s_ss["h2"], 1)
            x_transposed(0)
            act.wait_ge(s_attd, 1)
            nc.scalar.activation(atte, att, ACT.Exp).then_inc(s_atte, 1)
            u_out(0)
            act.wait_ge(s_ss["ctx"], 1)
            act.dma_start(cbias.rearrange("(b c) -> b c", c=C), ctxb).then_inc(s_cbias, 16)
            act.wait_ge(s_sp["mix0"], 1)
            nc.scalar.activation(mixn[:, 0:C // 2, :, :],
                                 row(ps_d[0][:, :].rearrange("p (o i) -> p o i", i=C), 2, BT), ACT.Copy).then_inc(s_ss["mix0"], 1)
            for g in range(0, MG, 2):
                act.wait_ge(s_mps, g + 1)
                nc.scalar.activation(mix_all[:, 4 * g:4 * g + 4, :].rearrange("p o b -> p (o b)"),
                                     ps_m[g % 4][:, :], ACT.Copy).then_inc(s_msa, 1)
            gate0_exp(0)
            for q in range(Q):
                act.wait_ge(s_wps, q + 1)
                nc.scalar.activation(wt_hi[:, q, :].rearrange("p (q m) -> p q m", q=Q),
                                     ps_d[q % 2][:, :].rearrange("p (m q) -> p q m", q=Q),
                                     ACT.Copy).then_inc(s_whi, 1)

            def step(s, par, k):
                def o_hi(t):
                    act.wait_ge(s_o1, s * NT + t + 1)
                    wait(act, s_mp, s * NT + max(t - 1, 0))
                    nc.scalar.activation(o1h[t % 2][:, :, :], o1[t % 2][:, :, :, :].rearrange("p q b c -> p q (b c)"),
                                         ACT.Copy).then_inc(s_o1h, 1)

                def ga_out(t):
                    act.wait_ge(s_gp, s * NT + t + 1)
                    if t == 0:
                        wait(act, s_h, s)
                    nc.scalar.activation(hs[:, t, :], ps_g[:, 0:G1], ACT.Copy)
                    nc.scalar.activation(tmp_all[:, bass.ds((s * NT + t) * ER1, ER1)], ps_g[:, G1:GC],
                                         ACT.Copy).then_inc(s_g, 1)

                def copies(n, base):
                    for i in range(base, base + n):
                        b, q = i // Q, i % Q
                        last = nc.scalar.activation(
                            xp[1 - par][C * q:C * q + C, b, :, 1:M + 1],
                            y_all[C * b:C * b + C, bass.ds((s + 1) * ST, ST)]
                            .rearrange("p (t q m) -> p t q m", t=NT, q=Q)[:, :, q, :], ACT.Copy)
                    return last

                if has(s, 1):
                    act.wait_ge(s_gtp, s + 2)
                    wait(act, s_dp, (s + 1) * NT)
                    nc.scalar.activation(gmT[:, :], ps_t[:, :], ACT.Copy).then_inc(s_gt, 1)
                if has(s, 0):
                    o_hi(0)
                    ga_out(0)
                if has(s, -1):
                    act.wait_ge(s_htp, s)
                    wait(act, s_rp, s - 1)
                    nc.scalar.activation(hT[:, :], ps_t[:, 0:P], ACT.Copy).then_inc(s_ht, 1)
                if has(s, 2):
                    x_transposed(s + 2)
                if has(s, 1):
                    act.wait_ge(s_x1, (s + 1) * NT + NT)
                    wait(act, s_cp, s * NT)
                    copies(3, 8)
                if has(s, 0):
                    o_hi(1)
                if has(s, 1):
                    copies(3, 11)
                if has(s, 0):
                    ga_out(1)
                if has(s, -1):
                    act.wait_ge(s_df1, s)
                    nc.scalar.activation(sc1[:, 2, :, :], sc1[:, 1, :, :], ACT.Exp).then_inc(s_ex1, 1)
                if has(s, 2):
                    u_out(s + 2)
                if has(s, 0):
                    o_hi(2)
                if has(s, 1):
                    copies(2, 14).then_inc(s_xpa, 1)
                if has(s, 0):
                    ga_out(2)
                if has(s, 2):
                    gate0_exp(s + 2)
                if has(s, 0):
                    o_hi(3)
                    ga_out(3)
            steps(act, step, -1, NS)

            def split(s, par, k):
                if has(s, 1):
                    act.wait_ge(s_ltp, s + 2)
                    wait(act, s_lp, s * NT)
                    nc.scalar.activation(lt_hi[1 - par][:, :], ps_a[1 - par][:, :], ACT.Copy).then_inc(s_lth, 1)
            steps(act, split, -1, NS - 1)

        @block.vector
        def _(dve):
            link, n = chain(dve, s_sd, 0)
            V = nc.vector
            qm = "p (m q) -> p q m"
            mq = "p (q m) -> p q m"

            def gates0(u):
                link, n = chain(dve, s_c0, u * N_C0)
                dve.wait_ge(s_vp, u + 1)
                dve.wait_ge(s_vb, u + 1)
                V.tensor_tensor(v[:, :, :], ps_v[:, 0:NT * UC].rearrange("p (t c) -> p t c", t=NT), vb[:, :, :],
                                ALU.add).then_inc(s_v, 1)
                dve.wait_ge(s_v, u + 1)
                lg = v[:, :, ER0:UC]
                link(V.reduce_max(small[:, 0, :], lg, AXX))
                V.tensor_tensor(sc0[:, 0, :, :], lg, row(small[:, 0, :], 2, E0), ALU.subtract).then_inc(s_df0, 1)
                link(V.tensor_tensor(pair0[:, 0], row(lg, 2, E0), row(lg, 3, E0), ALU.is_gt))
                link(V.tensor_tensor(pair0[:, 1], pair0[:, 0], row(upper[:, 0:E0, 0:E0], 1, NT), ALU.mult))
                link(V.reduce_sum(sc0[:, 2], pair0[:, 1], AXX))
                link(V.reduce_sum(sc0[:, 3], pair0[:, 1].rearrange("p t e j -> p t j e"), AXX))
                link(V.tensor_tensor(sc0[:, 4], sc0[:, 2], sc0[:, 3], ALU.subtract))
                link(V.tensor_tensor(sc0[:, 5], sc0[:, 4], row(sel0[:, :], 1, NT), ALU.is_lt))
                dve.wait_ge(s_ex0, u + 1)
                link(V.tensor_tensor(sc0[:, 6], sc0[:, 1], sc0[:, 5], ALU.mult))
                link(V.reduce_sum(small[:, 1, :], sc0[:, 6], AXX))
                link(V.reciprocal(small[:, 2, :], small[:, 1, :]))
                link(V.scalar_tensor_tensor(out=sc0[:, 7], in0=sc0[:, 6], scalar=SCALE0,
                                            in1=row(small[:, 2, :], 2, E0), op0=ALU.mult, op1=ALU.mult))
                link(V.tensor_tensor(gm[:, :, :].rearrange("p t (e r) -> p t e r", e=E0),
                                     v[:, :, 0:ER0].rearrange("p t (e r) -> p t e r", e=E0),
                                     row(sc0[:, 7], 3, R0), ALU.mult))
                wait(dve, s_gtp, u)
                link(V.tensor_copy(gms[:, :, 0, :].bitcast(fp32r), gm[:, :, :]))
                V.tensor_tensor(gms[:, :, 1, :], gm[:, :, :], gms[:, :, 0, :], ALU.subtract).then_inc(s_gm, 1)
                assert n[0] == N_C0, n[0]

            dve.wait_ge(s_sp["pm"], 1)
            V.tensor_copy(pm[:, :, :].rearrange("p c u -> p (c u)"), ps_d[0][:, 0:HC * UC]).then_inc(s_ss["pm"], 1)
            dve.wait_ge(s_sp["ctxT"], 1)
            V.tensor_copy(ctxT, ps_g[:, 0:C]).then_inc(s_ss["ctxT"], 1)
            dve.wait_ge(s_sp["att"], 1)
            dve.wait_ge(s_ld["mlp"], 96)
            link(V.tensor_tensor(att, ps_t[:, 0:K0], b2b, ALU.add))
            link(V.reduce_max(sm[:, 0:1], att, AXX))
            V.tensor_scalar(att, att, sm[:, 0:1], None, ALU.subtract).then_inc(s_attd, 1)
            dve.wait_ge(s_atte, 1)
            link(V.reduce_sum(sm[:, 1:2], atte, AXX))
            link(V.reciprocal(sm[:, 2:3], sm[:, 1:2]))
            V.tensor_scalar(att, atte, sm[:, 2:3], None, ALU.mult).then_inc(s_ss["att"], 1)
            dve.wait_ge(s_sp["attT"], 1)
            V.tensor_copy(attT, ps_v[0:K0, 0:P]).then_inc(s_ss["attT"], 1)
            dve.wait_ge(s_sp["rs"], 1)
            V.tensor_copy(rs[:, :], ps_c[:, 0:UC]).then_inc(s_ss["rs"], 1)
            dve.wait_ge(s_sp["ctx"], 1)
            dve.wait_ge(s_ld["ctx"], 32)
            V.tensor_tensor(ctxb, ps_g[:, 0:C], fsb, ALU.add).then_inc(s_ss["ctx"], 1)
            dve.wait_ge(s_sp["mix1"], 1)
            V.tensor_copy(mixn[:, C // 2:C, :, :], row(ps_d[1][:, :].rearrange("p (o i) -> p o i", i=C), 2, BT))\
             .then_inc(s_ss["mix1"], 1)
            dve.wait_ge(s_mbps, 1)
            for r in range(BT):
                last = V.tensor_copy(mixbias[C * r:C * r + C, :],
                                     ps_v[C * r:C * r + C, 128:128 + NB].rearrange("p (n r) -> p n r", r=BT)[:, :, r])
            last.then_inc(s_mbsb, 1)
            for g in range(1, MG, 2):
                dve.wait_ge(s_mps, g + 1)
                V.tensor_copy(mix_all[:, 4 * g:4 * g + 4, :].rearrange("p o b -> p (o b)"),
                              ps_m[g % 4][:, :]).then_inc(s_msd, 1)
            dve.wait_ge(s_sp["b"], 1)
            link(V.tensor_copy(b_hi[:, :].rearrange(mq, q=Q), ps_t[:, :].rearrange(qm, q=Q)))
            V.tensor_tensor(b_lo[:, :].rearrange(mq, q=Q), ps_t[:, :].rearrange(qm, q=Q),
                            b_hi[:, :].bitcast(fp32).rearrange(mq, q=Q), ALU.subtract).then_inc(s_ss["b"], 1)
            gates0(0)
            dve.wait_ge(s_sp["gw1"], 1)
            dve.wait_ge(s_zero, 4)
            for t in range(NT):
                V.tensor_copy(gw2bd[G1 * t:G1 * t + G1, t, :], ps_a[1][G1 * t:G1 * t + G1, Q * G1:Q * G1 + E1])
            V.tensor_copy(ga[:, :, 0:G1], ps_a[1][:, 0:Q * G1].rearrange("p (q g) -> p q g", q=Q))\
             .then_inc(s_ss["gw1"], 1)
            for q in range(Q):
                dve.wait_ge(s_whi, q + 1)
                V.tensor_tensor(wt_lo[:, q, :].rearrange(mq, q=Q), ps_d[q % 2][:, :].rearrange(qm, q=Q),
                                wt_hi[:, q, :].bitcast(fp32).rearrange(mq, q=Q), ALU.subtract).then_inc(s_wlo, 1)
            dve.wait_ge(s_ld["conv"], 16 * (C // CG))
            dve.wait_ge(s_const, 3)
            dve.wait_ge(s_zero, 1)
            for r in range(1, BT):
                V.tensor_copy(cwt[C * r:C * r + C, :, :], cwt[0:C, :, :])
            link(V.tensor_reduce(gmask, gq.rearrange("p r g -> p g r"), axis=AXX, op=ALU.add))
            for q in range(Q):
                part = slice(C * q, C * q + C)
                for j in range(SH):
                    ps = [p for p in range(Q) if 0 <= 4 * j + q - p < TAPS]
                    if not ps:
                        continue
                    for p in ps:
                        kk = 4 * j + q - p
                        last = V.tensor_tensor(
                            cw[part, j, p, :].rearrange("i (g o) -> i g o", o=CG),
                            row(cwt[part, :, kk], 1, C // CG), row(gmask[part, :], 2, CG), ALU.mult)
            last.then_inc(s_cw, 1)
            dve.wait_ge(s_ld["lora"], 16)
            link(V.tensor_copy(lb_hi[:, :].rearrange(mq, q=Q), lbn.rearrange(qm, q=Q)))
            V.tensor_tensor(lb_lo[:, :].rearrange(mq, q=Q), lbn.rearrange(qm, q=Q),
                            lb_hi[:, :].bitcast(fp32).rearrange(mq, q=Q), ALU.subtract).then_inc(s_lb, 1)
            dve.wait_ge(s_ld["rows"], 16 * 4)

            def step(s, par, k):
                def o_out(t):
                    dve.wait_ge(s_cp, s * NT + t + 1)
                    wait(dve, s_gp, s * NT + max(t - 1, 0))
                    wait(dve, s_o1l, s * NT + max(t - 1, 0))
                    if t == 0:
                        dve.wait_ge(s_bias[par], 16 * (k + 1))
                    V.tensor_tensor(o1[t % 2][:, :, :, :].rearrange("m p b o -> m b p o"),
                                    ps_c[:, :].rearrange("m (b p o) -> m b p o", b=BT, p=Q),
                                    row(bias[par][:, t, :, :], 2, Q), ALU.add).then_inc(s_o1, 1)

                def y_out(t):
                    dve.wait_ge(s_mp, s * NT + t + 1)
                    yt = y_all[:, bass.ds(s * ST + t * H, H)]
                    V.tensor_tensor(yt, ps_d[t % 2][:, :], yt, ALU.add).then_inc(s_y, 1)

                def x1_out(t):
                    dve.wait_ge(s_dp, (s + 1) * NT + t + 1)
                    V.tensor_tensor(y_all[:, bass.ds((s + 1) * ST + t * H, H)].rearrange("p (q m) -> p q m", q=Q),
                                    ps_d[t % 2][:, :].rearrange("p (q m) -> p q m", q=Q),
                                    xs[1 - par][:, t, :].rearrange("p (m q) -> p q m", q=Q), ALU.add)\
                     .then_inc(s_x1, 1)

                def copies(n, base):
                    for i in range(base, base + n):
                        b, q = i // Q, i % Q
                        last = V.tensor_scalar(
                            xp[1 - par][C * q:C * q + C, b, :, 1:M + 1],
                            y_all[C * b:C * b + C, bass.ds((s + 1) * ST, ST)]
                            .rearrange("p (t q m) -> p t q m", t=NT, q=Q)[:, :, q, :], 1.0, None, ALU.mult)
                    return last

                if has(s, 0):
                    o_out(0)
                if has(s, 1):
                    for t in range(NT):
                        x1_out(t)
                    dve.wait_ge(s_x1, (s + 1) * NT + NT)
                    wait(dve, s_cp, s * NT)
                    copies(2, 0)
                if has(s, 0):
                    o_out(1)
                if has(s, 1):
                    copies(3, 2)
                if has(s, 0):
                    y_out(0)
                if has(s, -1):
                    link, n = chain(dve, s_c2, (s - 1) * N_C2)
                    dve.wait_ge(s_rp, s)
                    V.tensor_tensor(sc1[:, 0], ps_v[:, 0:NT * E1].rearrange("p (t e) -> p t e", t=NT),
                                    row(gb2_b[:, :], 1, NT), ALU.add).then_inc(s_r, 1)
                    dve.wait_ge(s_r, s)
                    link(V.reduce_max(small[:, 4, :], sc1[:, 0], AXX))
                    V.tensor_tensor(sc1[:, 1], sc1[:, 0], row(small[:, 4, :], 2, E1), ALU.subtract).then_inc(s_df1, 1)
                    link(V.tensor_tensor(pair1[:, 0], row(sc1[:, 0], 2, E1), row(sc1[:, 0], 3, E1), ALU.is_gt))
                    link(V.tensor_tensor(pair1[:, 1], pair1[:, 0], row(upper[:, :, :], 1, NT), ALU.mult))
                    link(V.reduce_sum(sc1[:, 3], pair1[:, 1], AXX))
                    link(V.reduce_sum(sc1[:, 4], pair1[:, 1].rearrange("p t e j -> p t j e"), AXX))
                    link(V.tensor_tensor(sc1[:, 5], sc1[:, 3], sc1[:, 4], ALU.subtract))
                    link(V.tensor_tensor(oh[:, :, :, :], row(sc1[:, 5], 2, 2), row(sel1[:, :, :], 1, NT),
                                         ALU.is_equal))
                    link(V.reduce_sum(cnt1[:, :, :], oh[:, :, :, :].rearrange("p t c e -> p c e t"), AXX))
                    link(V.tensor_tensor(cnt[:, :, :], cnt[:, :, :], cnt1[:, :, :], ALU.add))
                    dve.wait_ge(s_ex1, s)
                    link(V.tensor_tensor(exs1[:, :, :, :], row(sc1[:, 2], 2, 2), oh[:, :, :, :], ALU.mult))
                    exf = exs1[:, :, :, :].rearrange("p t c e -> p t (c e)")
                    link(V.reduce_sum(small[:, 5, :], exf, AXX))
                    link(V.reciprocal(small[:, 6, :], small[:, 5, :]))
                    link(V.tensor_scalar(small[:, 7, :], small[:, 6, :], ALPHA, None, ALU.mult))
                    link(V.tensor_tensor(
                        wst_all[:, bass.ds((s - 1) * NT, NT), :, :].rearrange("p t c e -> p t (c e)"), exf,
                        row(small[:, 7, :], 2, 2 * E1), ALU.mult))
                    assert n[0] == N_C2, n[0]
                if has(s, 0):
                    o_out(2)
                if has(s, 1):
                    copies(3, 5).then_inc(s_xpd, 1)
                if has(s, 0):
                    y_out(1)
                if has(s, 2):
                    gates0(s + 2)
                if has(s, 0):
                    o_out(3)
                    y_out(2)
                    link, n = chain(dve, s_c1, s * N_C1)
                    dve.wait_ge(s_g, s * NT + NT)
                    link(V.tensor_tensor(ha[:, :, :], hs[:, :, :], row(gb1_b[:, :], 1, NT), ALU.add))
                    link(V.reduce_sum(small[:, 12, :], ha[:, :, :], AXX))
                    link(V.tensor_scalar(small[:, 13, :], small[:, 12, :], 1.0 / G1, None, ALU.mult))
                    link(V.tensor_tensor(hb[:, :, :], ha[:, :, :], row(small[:, 13, :], 2, G1), ALU.subtract))
                    link(V.tensor_tensor(ha[:, :, :], hb[:, :, :], hb[:, :, :], ALU.mult))
                    link(V.reduce_sum(small[:, 14, :], ha[:, :, :], AXX))
                    V.tensor_scalar(small[:, 15, :], small[:, 14, :], 1.0 / G1, EPS, ALU.mult, ALU.add)\
                     .then_inc(s_var, 1)
                    y_out(3)
                    dve.wait_ge(s_rstd, s + 1)
                    link(V.tensor_tensor(ha[:, :, :], hb[:, :, :], row(small[:, 16, :], 2, G1), ALU.mult))
                    link(V.tensor_tensor(hb[:, :, :], ha[:, :, :], row(gamma_b[:, :], 1, NT), ALU.mult))
                    link(V.tensor_tensor(ha[:, :, :], hb[:, :, :], row(beta_b[:, :], 1, NT), ALU.add))
                    wait(dve, s_htp, s)
                    V.tensor_scalar(hr[:, :, :], ha[:, :, :], 0.0, None, ALU.max).then_inc(s_h, 1)
                    assert n[0] == N_C1, n[0]
            steps(dve, step, -1, NS)

            V.tensor_copy(cnt1[:, :, :], cnt[:, :, :]).then_inc(s_cnt, 1)
            link, n = chain(dve, s_c3, 0)
            dve.wait_ge(s_cntp, 1)
            link(V.tensor_scalar(allowed[:, :, :], ps_v[:, 0:2 * E1].rearrange("p (c e) -> p c e", c=2),
                                 float(CAPACITY), None, ALU.is_le))
            link(V.tensor_tensor(wst_all[:, :, :, :], wst_all[:, :, :, :], row(allowed[:, :, :], 1, NS * NT),
                                 ALU.mult))
            V.tensor_tensor(wst_all[:, :, 0, :], wst_all[:, :, 0, :], wst_all[:, :, 1, :], ALU.add).then_inc(s_w, 1)

            dve.wait_ge(s_y, NS * NT)

            def finish(s, par, k):
                if has(s, 1):
                    dve.wait_ge(s_lth, s + 2)
                    V.tensor_tensor(lt_lo[1 - par][:, :], ps_a[1 - par][:, :], lt_hi[1 - par][:, :].bitcast(fp32),
                                    ALU.subtract).then_inc(s_ltl, 1)
                if has(s, 0):
                    for t in range(NT):
                        dve.wait_ge(s_lp, s * NT + t + 1)
                        wait(dve, s_out[t], s * 16)
                        V.tensor_tensor(yo[t].rearrange(qm, q=Q), ps_l[t][:, :].rearrange(mq, q=Q),
                                        y_all[:, bass.ds(s * ST + t * H, H)].rearrange(mq, q=Q),
                                        ALU.add).then_inc(s_yo[t], 1)
            steps(dve, finish, -1, NS - 1)

        @block.tensor
        def _(pe):
            T = nc.tensor
            idp = ident[:, :]

            def t1(u, bank_x, t):
                for c in range(HC):
                    last = T.transpose(ps_a[t % 2][:, c * P:(c + 1) * P], bank_x[:, t, c * P:(c + 1) * P], idp)
                last.then_inc(s_xtp, 1)

            def u_products(u):
                pe.wait_ge(s_xt, u * NT + NT)
                for t in range(NT):
                    for c in range(HC):
                        last = T.matmul(ps_a[0][:, t * UC:(t + 1) * UC], xT[:, t, c, :], pm[:, c, :],
                                        start=(c == 0), stop=(c == HC - 1))
                last.then_inc(s_up, 1)

            def mix(u):
                pe.wait_ge(s_u, u + 1)
                pe.wait_ge(s_bd, u + 1)
                wait(pe, s_v, u)
                wait(pe, s_r, u - 2)
                for t in range(NT):
                    last = T.matmul(ps_v[:, t * UC:(t + 1) * UC],
                                    mixbd[:, t, :, :].rearrange("p r o -> p (r o)"), u_sb[:, t, :],
                                    start=True, stop=True)
                last.then_inc(s_vp, 1)

            pe.wait_ge(s_const, 1)
            pe.wait_ge(s_ld["cond"], 16)
            T.transpose(ps_c[:, 0:P], condn, idp).then_inc(s_sp["condT"], 1)
            pe.wait_ge(s_ld["aw"], 32)
            for c in range(HC):
                last = T.transpose(ps_d[0][:, c * UC:(c + 1) * UC], aw[:, c * P:(c + 1) * P], ident[0:UC, 0:UC])
            last.then_inc(s_sp["pm"], 1)
            pe.wait_ge(s_ld["mlp"], 96)
            pe.wait_ge(s_ss["condT"], 1)
            T.matmul(ps_t[:, 0:P], w0n, condT, start=True, stop=True).then_inc(s_sp["h1"], 1)
            pe.wait_ge(s_x[0], 16)
            t1(0, xs[0], 0)
            t1(0, xs[0], 1)
            pe.wait_ge(s_ss["h1"], 1)
            T.matmul(ps_t[:, 0:P], w1n, h1, start=True, stop=True).then_inc(s_sp["h2"], 1)
            pe.wait_ge(s_ld["ctx"], 32)
            T.transpose(ps_g[:, 0:C], ctxn, ident[0:C, 0:C]).then_inc(s_sp["ctxT"], 1)
            pe.wait_ge(s_ss["h2"], 1)
            T.matmul(ps_t[:, 0:K0], h2, w2n, start=True, stop=True).then_inc(s_sp["att"], 1)
            for t in (2, 3):
                pe.wait_ge(s_xt, t - 1)
                t1(0, xs[0], t)
            pe.wait_ge(s_ss["pm"], 1)
            for c in range(HC):
                last = T.matmul(ps_c[:, 0:UC], ones[:, :], pm[:, c, :], start=(c == 0), stop=(c == HC - 1))
            last.then_inc(s_sp["rs"], 1)
            pe.wait_ge(s_ss["ctxT"], 1)
            T.matmul(ps_g[:, 0:C], condT, ctxT, start=True, stop=True).then_inc(s_sp["ctx"], 1)
            pe.wait_ge(s_ss["att"], 1)
            T.transpose(ps_v[0:K0, 0:P], att, idp).then_inc(s_sp["attT"], 1)
            pe.wait_ge(s_ss["attT"], 1)
            pe.wait_ge(s_ld["mixw"], 16)
            for i in range(2):
                T.matmul(ps_d[i][:, :], attT, wk[:, i * (C // 2):(i + 1) * (C // 2), :].rearrange("k o i -> k (o i)"),
                         start=True, stop=True).then_inc(s_sp[f"mix{i}"], 1)
            pe.wait_ge(s_ld["mixb"], 16)
            T.matmul(ps_v[:, P:P + NB], mbn.rearrange("k r o -> k (r o)"), attT, start=True, stop=True).then_inc(s_mbps, 1)
            u_products(0)
            for g in range(MG):
                if g < 4:
                    pe.wait_ge(s_ss[("rs", "ctx", "mix0", "mix1")[g]], 1)
                elif g % 2 == 0:
                    pe.wait_ge(s_msa, g // 2 - 1)
                else:
                    pe.wait_ge(s_msd, g // 2 - 1)
                pe.wait_ge(s_ss["mix0" if g < MG // 2 else "mix1"], 1)
                for o in range(4):
                    last = T.transpose(ps_m[g % 4][:, o * NB:(o + 1) * NB], mixn[:, 4 * g + o, :, :].rearrange("b r i -> b (r i)"), idp)
                last.then_inc(s_mps, 1)
            pe.wait_ge(s_bn, 1)
            for c in range(HC):
                last = T.transpose(ps_t[:, c * P:(c + 1) * P], bn2[:, c, :, :].rearrange("p d e -> p (d e)"), idp)
            last.then_inc(s_sp["b"], 1)
            pe.wait_ge(s_ld["gate"], 32)
            for q in range(Q):
                last = T.transpose(ps_a[1][:, q * G1:(q + 1) * G1],
                                   gw1n.rearrange("p (m q) -> p q m", q=Q)[:, q, :], ident[0:G1, 0:G1])
            T.transpose(ps_a[1][:, Q * G1:Q * G1 + E1], gw2n.rearrange("e t c -> e (t c)"), ident[0:E1, 0:E1])\
             .then_inc(s_sp["gw1"], 1)
            pe.wait_ge(s_mbsb, 1)
            mix(0)
            pe.wait_ge(s_ld["w"], 16)
            for q in range(Q):
                if q == 0:
                    pe.wait_ge(s_msa, MG // 2)
                elif q == 1:
                    pe.wait_ge(s_msd, MG // 2)
                else:
                    pe.wait_ge(s_wlo, q - 1)
                for c in range(HC):
                    last = T.transpose(ps_d[q % 2][:, c * P:(c + 1) * P],
                                       wn[:, c, :].rearrange("p (m q) -> p q m", q=Q)[:, q, :], idp)
                last.then_inc(s_wps, 1)
            pe.wait_ge(s_ss["gw1"], 1)

            def step(s, par, k):
                def conv(t):
                    if t == 0:
                        pe.wait_ge(s_xpd, s + 1)
                        pe.wait_ge(s_xpa, s + 1)
                    wait(pe, s_o1, s * NT + t)
                    for b in range(BT):
                        for j in range(SH):
                            last = T.matmul(ps_c[:, b * P:(b + 1) * P], xp[par][:, b, t, j:j + M],
                                            cw[:, j, :, :].rearrange("p q o -> p (q o)"),
                                            start=(j == 0), stop=(j == SH - 1))
                    last.then_inc(s_cp, 1)

                def gates(t):
                    pe.wait_ge(s_o1, s * NT + t + 1)
                    wait(pe, s_g, s * NT + t)
                    for q in range(Q):
                        last = T.matmul(ps_g[:, 0:GC], o1[t % 2][:, q, :, :].rearrange("p b c -> p (b c)"),
                                        ga[:, q, :], start=(q == 0), stop=(q == Q - 1))
                    last.then_inc(s_gp, 1)

                def main(t):
                    pe.wait_ge(s_o1l, s * NT + t + 1)
                    if t < 2 and has(s, 1):
                        pe.wait_ge(s_x1, (s + 1) * NT + 3 + t)
                    else:
                        wait(pe, s_y, s * NT + t - 1)
                    n = 0
                    for q in range(Q):
                        for a, w in ((o1h, wt_hi), (o1h, wt_lo), (o1l, wt_hi)):
                            last = T.matmul(ps_d[t % 2][:, :], a[t % 2][:, q, :], w[:, q, :],
                                            start=(n == 0), stop=(n == 3 * Q - 1))
                            n += 1
                    last.then_inc(s_mp, 1)

                def delta(t):
                    if t < 2:
                        wait(pe, s_y, s * NT)
                        wait(pe, s_x1, s * NT + NT)
                    else:
                        pe.wait_ge(s_x1, (s + 1) * NT + t - 1)
                    lhs = gmT[:, t * P:(t + 1) * P]
                    T.matmul(ps_d[t % 2][:, :], lhs, b_hi[:, :], start=True, stop=False)
                    T.matmul(ps_d[t % 2][:, :], lhs, b_lo[:, :], start=False, stop=True).then_inc(s_dp, 1)

                if isinstance(s, int) and s == 0:
                    pe.wait_ge(s_cw, 1)
                    pe.wait_ge(s_zero, 4)
                    pe.wait_ge(s_ld["lora_a"], 16 * E1)
                if has(s, 0):
                    conv(0)
                if has(s, 1):
                    pe.wait_ge(s_gm, s + 2)
                    wait(pe, s_ht, s - 1)
                    for t in range(NT):
                        last = T.transpose(ps_t[:, t * P:(t + 1) * P],
                                           gms[:, t, :, :].rearrange("p a c -> p (a c)"), idp)
                    last.then_inc(s_gtp, 1)
                if has(s, 0):
                    gates(0)
                if has(s, -1):
                    pe.wait_ge(s_h, s)
                    pe.wait_ge(s_gt, upto(s + 2, NS))
                    T.transpose(ps_t[:, 0:P], hr[:, :, :].rearrange("p t g -> p (t g)"), idp).then_inc(s_htp, 1)
                if has(s, 1):
                    pe.wait_ge(s_gt, s + 2)
                    if isinstance(s, int) and s == -1:
                        pe.wait_ge(s_wlo, Q)
                    delta(0)
                    delta(1)
                if has(s, -1):
                    pe.wait_ge(s_ht, s)
                    pe.wait_ge(s_v, upto(s + 2, NS))
                    T.matmul(ps_v[:, 0:NT * E1], hT[:, :], gw2bd[:, :, :].rearrange("p t e -> p (t e)"),
                             start=True, stop=True).then_inc(s_rp, 1)
                if has(s, 1):
                    delta(2)
                    delta(3)
                if has(s, 2):
                    pe.wait_ge(s_x[par], 16 * (k + 2))
                    for t in range(NT):
                        if t == 0:
                            wait(pe, s_u, s + 2)
                        wait(pe, s_xt, (s + 2) * NT + max(t - 1, 0))
                        t1(s + 2, xs[par], t)
                if has(s, 0):
                    conv(1)
                    main(0)
                    gates(1)
                if has(s, 2):
                    u_products(s + 2)
                if has(s, 0):
                    conv(2)
                    main(1)
                if has(s, 2):
                    mix(s + 2)
                if has(s, 0):
                    gates(2)
                    conv(3)
                    if has(s, 1):
                        main(2)
                        gates(3)
                    else:
                        gates(3)
                        main(2)
                    main(3)
            steps(pe, step, -1, NS)

            pe.wait_ge(s_cnt, 1)
            T.matmul(ps_v[:, 0:2 * E1], ones[:, :], cnt1[:, :, :].rearrange("p c e -> p (c e)"),
                     start=True, stop=True).then_inc(s_cntp, 1)
            pe.wait_ge(s_lb, 1)

            def lora(s, par, k):
                if has(s, 1):
                    pe.wait_ge(s_lt, s + 2)
                    wait(pe, s_ltl, s)
                    for t in range(NT):
                        last = T.transpose(ps_a[1 - par][:, t * P:(t + 1) * P],
                                           ltw[1 - par][:, t * P:(t + 1) * P], idp)
                    last.then_inc(s_ltp, 1)
                if has(s, 0):
                    pe.wait_ge(s_ltl, s + 1)
                    for t in range(NT):
                        wait(pe, s_yo[t], s)
                        for n, (a, w) in enumerate(((lt_hi, lb_hi), (lt_hi, lb_lo), (lt_lo, lb_hi))):
                            last = T.matmul(ps_l[t][:, :], a[par][:, t * P:(t + 1) * P], w[:, :],
                                            start=(n == 0), stop=(n == 2))
                        last.then_inc(s_lp, 1)
            steps(pe, lora, -1, NS - 1)


_INS = ['x', 'cond_128', 'fside_S_0', 'L0_cond_W0', 'L0_cond_b0', 'L0_cond_W1', 'L0_cond_b1', 'L0_cond_W2',
        'L0_cond_b2', 'L0_cond_weight', 'L0_cond_bias_k', 'L0_ffn_A', 'L0_ffn_B', 'L0_ffn_Wr', 'L1_cond_weight',
        'L1_cond_c_weight', 'L1_ffn_weight', 'L1_ffn_lora_A', 'L1_ffn_lora_B', 'L1_ffn_gw1', 'L1_ffn_gb1',
        'L1_ffn_ln_gamma', 'L1_ffn_ln_beta', 'L1_ffn_gw2', 'L1_ffn_gb2']


def kernel(**inputs):
    import numpy as _np
    import concourse.bacc as _bacc
    from concourse import mybir as _mybir
    from concourse.bass_utils import run_bass_kernel_spmd as _run

    nc = _bacc.Bacc("TRN2", target_bir_lowering=False, num_devices=1)
    arrays, args = {}, []
    for name in _INS:
        a = _np.ascontiguousarray(inputs[name])
        arrays[f"in_{name}_dram"] = a
        args.append(nc.dram_tensor(f"in_{name}_dram", a.shape, _mybir.dt.from_np(a.dtype), kind="ExternalInput").ap())
    shape = _np.shape(inputs['x'])
    args.append(nc.dram_tensor("out_dram", shape, _mybir.dt.float32, kind="ExternalOutput").ap())
    adaln_ffn_kernel(nc, *args)
    r = _run(nc, [arrays], core_ids=[0])
    return r.results[0]["out_dram"]
```

```python
import concourse.bass as bass
from concourse import mybir
from contextlib import ExitStack



def adaln_ffn_kernel(nc: bass.Bass, x, cond, fside, w0, b0, w1, b1, w2, b2, mixw, mixb, ffa, ffb, ffr,
                     convw, ctxw, wmain, lora_a, lora_b, gw1, gb1, gamma, beta, gw2, gb2, out):
    fp32 = mybir.dt.float32
    fp32r = mybir.dt.float32r
    ALU = mybir.AluOpType
    ACT = mybir.ActivationFunctionType
    AXX = mybir.AxisListType.X

    P = 128
    NB, C, H = x.shape
    K0 = mixw.shape[0]
    E0, R0 = ffa.shape[0], ffa.shape[1]
    ER0 = E0 * R0
    UC = ER0 + E0
    SCALE0 = 16.0 / float(R0) ** 0.5
    E1, R1 = lora_a.shape[0], lora_a.shape[2]
    ER1 = E1 * R1
    G1 = gw1.shape[0]
    GC = G1 + ER1
    MC = (H + GC) // 2
    TAPS = convw.shape[2]
    CG = convw.shape[1]
    CAPACITY = int(3.0 * NB * C / E1)
    ALPHA = 1.0 / R1
    EPS = 1e-05
    BT = P // C
    NT = 4
    NS = NB // (BT * NT)
    Q = 4
    M = H // Q
    HC = H // P
    SH = 3
    ST = NT * H

    x_v = x.rearrange("(s t b) c h -> s (b c) t h", t=NT, b=BT)
    out_v = out.rearrange("(n b) c h -> n (b c) h", b=BT)

    ctx = ExitStack()
    with ctx:
        def sb(name, shape, dt=fp32):
            return ctx.enter_context(nc.sbuf_tensor(name, shape, dt))

        def sem(name):
            return ctx.enter_context(nc.semaphore(name))

        def row(v, axis, n):
            v = v.unsqueeze(axis)
            shape = list(v.shape)
            shape[axis] = n
            return v.broadcast_to(shape)

        def wait(eng, s, value):
            if not isinstance(value, int) or value > 0:
                eng.wait_ge(s, value)

        y_all = sb("y_all", [P, NS * ST])
        tmp_all = sb("tmp_all", [P, NS * NT * ER1])
        wst_all = sb("wst_all", [P, NS * NT, 2, E1])
        mix_all = sb("mix_all", [P, C, NB])
        wt_hi = sb("wt_hi", [P, Q, H + GC], fp32r)
        wt_lo = sb("wt_lo", [P, Q, H + GC], fp32r)
        xs = [sb(f"xs{i}", [P, NT, H]) for i in range(2)]
        xT = sb("xT", [P, NT, HC, P])
        xp = [sb(f"xp{i}", [P, BT, NT, M + 2]) for i in range(2)]
        o1 = [sb(f"o1_{i}", [P, Q, BT, C]) for i in range(2)]
        o1h = [sb(f"o1h{i}", [P, Q, P], fp32r) for i in range(2)]
        o1l = [sb(f"o1l{i}", [P, Q, P], fp32r) for i in range(2)]
        bias = [sb(f"bias{i}", [P, NT, BT, C]) for i in range(2)]
        mixbd = sb("mixbd", [P, NT, BT, C])
        mixbias = sb("mixbias", [P, NS * NT])
        pm = sb("pm", [P, HC, UC])
        rs = sb("rs", [P, UC])
        b_hi = sb("b_hi", [P, H], fp32r)
        b_lo = sb("b_lo", [P, H], fp32r)
        ga = sb("ga", [P, Q, GC])
        cw = sb("cw", [P, SH, Q, C])
        lb_hi = sb("lb_hi", [P, H], fp32r)
        lb_lo = sb("lb_lo", [P, H], fp32r)
        gw2bd = sb("gw2bd", [P, NT, E1])
        ident = sb("ident", [P, P])
        ones = sb("ones", [P, P])
        u_sb = sb("u_sb", [P, NT, UC])
        vb = sb("vb", [P, NT, UC])
        v = sb("v", [P, NT, UC])
        gms = sb("gms", [P, NT, 2, ER0])
        gm = sb("gm", [P, NT, ER0])
        gmT = sb("gmT", [P, NT * P], fp32r)
        hs = sb("hs", [P, NT, G1])
        ha = sb("ha", [P, NT, G1])
        hb = sb("hb", [P, NT, G1])
        hr = sb("hr", [P, NT, G1])
        hT = sb("hT", [P, P])
        gb1_b = sb("gb1_b", [P, G1])
        gamma_b = sb("gamma_b", [P, G1])
        beta_b = sb("beta_b", [P, G1])
        gb2_b = sb("gb2_b", [P, E1])
        repmask = sb("repmask", [P, BT])
        upper = sb("upper", [P, E1, E1])
        sel0 = sb("sel0", [P, E0])
        sel1 = sb("sel1", [P, 2, E1])
        mhalf = sb("mhalf", [P, NT])
        small = sb("small", [P, 17, NT])
        sc0 = sb("sc0", [P, 8, NT, E0])
        pair0 = sb("pair0", [P, 2, NT, E0, E0])
        sc1 = sb("sc1", [P, 6, NT, E1])
        oh = sb("oh", [P, NT, 2, E1])
        exs1 = sb("exs1", [P, NT, 2, E1])
        pair1 = sb("pair1", [P, NT, E1, E1])
        cnt = sb("cnt", [P, 2, E1])
        cnt1 = sb("cnt1", [P, 2, E1])
        allowed = sb("allowed", [P, 2, E1])

        at = [2 * ST]

        def early(parts, shape):
            n = 1
            for d in shape:
                n *= d
            a = y_all[0:parts, at[0]:at[0] + n]
            at[0] += n
            assert at[0] <= NS * ST
            if len(shape) == 1:
                return a
            names = "abcd"[:len(shape)]
            return a.rearrange(f"p ({' '.join(names)}) -> p {' '.join(names)}",
                               **{k: d for k, d in zip(names[1:], shape[1:])})

        wn = early(P, [HC, H])
        wk = early(K0, [C, C])
        mixn = early(P, [C, BT, C])
        bn = early(P, [HC, ER0])
        bn2 = early(P, [HC, 2, ER0])
        aw = early(UC, [H])
        gw1n = early(G1, [H])
        gw2n = early(E1, [NT, G1])
        lbn = early(P, [H])
        condn = early(P, [P])
        w0n = early(P, [P])
        w1n = early(P, [P])
        condT = early(P, [P])
        h1 = early(P, [P])
        h2 = early(P, [P])
        w2n = early(P, [K0])
        b0c = early(P, [1])
        b1c = early(P, [1])
        b2b = early(P, [K0])
        mbn = early(K0, [BT, C])
        ctxn = early(C, [P])
        ctxT = early(P, [C])
        ctxb = early(P, [C])
        fsb = early(P, [C])
        cwt = early(C, [CG, TAPS])
        taps = early(P, [CG, Q * SH])
        att = early(P, [K0])
        atte = early(P, [K0])
        attT = early(K0, [P])
        gq = early(P, [BT, C // CG])
        gmask = early(P, [C // CG])
        sm = early(P, [4])

        def pb(name):
            return ctx.enter_context(nc.psum_tensor(name, [P, 512], fp32))

        ps_a = [pb("ps_a0"), pb("ps_a1")]
        ps_t = pb("ps_t")
        ps_v = pb("ps_v")
        ps_d = [pb("ps_d0"), pb("ps_d1")]
        ps_c = pb("ps_c")
        ps_g = pb("ps_g")

        cbias = nc.dram_tensor("cbias", (NB * C,), fp32).ap()

        s_x = [sem(f"x_loaded{i}") for i in range(2)]
        s_xf = sem("x_first_half_loaded")
        s_bias = [sem(f"bias_loaded{i}") for i in range(2)]
        s_ld = {n: sem(f"ld_{n}") for n in ("cond", "w0", "w1", "w2", "b0", "b1", "b2", "side", "aw", "mixw", "mixb",
                                            "bn", "w", "gate", "ctx", "conv", "lora", "lora_a", "rows")}
        s_cbias = sem("cbias_stored")
        s_id = sem("ident_steps")
        s_const = sem("consts_ready")
        s_zero = sem("zeros_ready")
        names = ("condT", "pm", "h1", "ctxT", "b", "h2", "gw1", "att", "ctx", "rs", "attT", "mix0", "mix1")
        s_sp = {n: sem(f"setup_ps_{n}") for n in names}
        s_ss = {n: sem(f"setup_sb_{n}") for n in names}
        s_wps, s_whi, s_wlo = sem("w_ps"), sem("w_hi"), sem("w_lo")
        s_mps, s_msa, s_msd = sem("mix_ps"), sem("mix_copied_act"), sem("mix_copied_dve")
        s_mbps, s_mbsb = sem("mixbias_ps"), sem("mixbias_sb")
        s_cw, s_bn = sem("convw_ready"), sem("b_doubled")
        s_lb = sem("lora_b_split")
        s_gah, s_gal = sem("ga_hi"), sem("ga_lo")
        s_sd = sem("setup_chain")
        s_attd, s_atte = sem("att_shifted"), sem("att_exp")

        s_xtp, s_xt = sem("xT_ps"), sem("xT_copied")
        s_up, s_u = sem("u_ps"), sem("u_copied")
        s_bd, s_vb = sem("mixbd_ready"), sem("vbias_ready")
        s_vp, s_v = sem("v_ps"), sem("v_ready")
        s_df0, s_ex0 = sem("gate0_shifted"), sem("gate0_exp")
        s_c0 = sem("gate0_chain")
        s_gm, s_gtp, s_gt = sem("gm_ready"), sem("gmT_ps"), sem("gmT_copied")
        s_dp, s_x1 = sem("delta_ps"), sem("x1_ready")
        s_xpd, s_xpa, s_xph = sem("xp_dve"), sem("xp_act"), sem("xp_first_half")
        s_cp, s_o1 = sem("conv_ps"), sem("o1_ready")
        s_o1h, s_o1l = sem("o1_hi"), sem("o1_lo")
        s_gp, s_g = sem("ga_ps"), sem("ga_copied")
        s_ma, s_mp, s_y = sem("main_first_half_ps"), sem("main_ps"), sem("y_ready")
        s_c1 = sem("norm_chain")
        s_var, s_rstd = sem("var_ready"), sem("rstd_ready")
        s_h, s_htp, s_ht = sem("hidden_ready"), sem("hT_ps"), sem("hT_copied")
        s_rp, s_r = sem("router_ps"), sem("router_read")
        s_df1, s_ex1 = sem("gate1_shifted"), sem("gate1_exp")
        s_c2 = sem("gate1_chain")
        s_cnt, s_cntp, s_w = sem("counts_ready"), sem("counts_ps"), sem("weights_ready")
        s_c3 = sem("allowed_chain")
        s_lt, s_ltp = sem("weighted"), sem("weighted_ps")
        s_lth, s_ltl = sem("weightedT_hi"), sem("weightedT_lo")
        s_lp, s_yo = sem("lora_ps"), [sem(f"out_ready{i}") for i in range(NT)]
        s_out = [[sem(f"out_stored{i}_{t}") for t in range(NT)] for i in range(2)]
        s_ltf = sem("first_weightedT_lo")

        ltw = [xs[0][:, i, :] for i in range(2)]
        lt = [xs[1][:, i, :] for i in range(2)]
        lt_hi = [wt_hi[:, i, 0:H] for i in range(2)]
        lt_lo = [wt_lo[:, i, 0:H] for i in range(2)]
        yo = [[xT[:, t, :, :].rearrange("p c m -> p (c m)") for t in range(NT)],
              [xp[0][:, :, :, :].rearrange("p b t m -> p (b t m)")[:, t * H:(t + 1) * H] for t in range(NT)]]
        ps_l = [ps_c, ps_g, ps_d[0], ps_d[1]]

        ps_w = [ps_a[0], ps_a[1], ps_d[0], ps_d[1]]
        ps_m = [ps_c, ps_g, ps_d[0], ps_d[1]]
        MG = C // 4
        GWC = NT * UC

        def chain(eng, s, base):
            n = [0]

            def link(ins, now=True):
                n[0] += 1
                ins.then_inc(s, 1)
                if now:
                    eng.wait_ge(s, base + n[0])
            return link, n

        def shifted(i, u, into, first=0, tiles=NT):
            b, q = i // Q, i % Q
            return (into[C * q:C * q + C, b, first:first + tiles, 1:M + 1],
                    y_all[C * b:C * b + C, bass.ds(u * ST + first * H, tiles * H)]
                    .rearrange("p (t q m) -> p t q m", t=tiles, q=Q)[:, :, q, :])

        EARLY_DVE = 10

        N_C0, N_C1, N_C2 = 13, 8, 13
        N_C1A = 6

        def steps(eng, step, first, last):
            for s in range(first, 2):
                step(s, s % 2, s // 2)
            with eng.Fori(1, NS // 2 - 1) as k:
                step(k * 2, 0, k)
                step(k * 2 + 1, 1, k)
            for s in range(NS - 2, last + 1):
                step(s, s % 2, s // 2)

        def has(s, ahead):
            return not isinstance(s, int) or 0 <= s + ahead < NS

        def at_step(s, n):
            return isinstance(s, int) and s == n

        def upto(count, most):
            return min(count, most) if isinstance(count, int) else count

        block = ctx.enter_context(nc.Block())

        @block.sync
        def _(sp):
            sp.dma_start(condn, cond).then_inc(s_ld["cond"], 16)
            sp.dma_start(w0n, w0).then_inc(s_ld["w0"], 16)
            sp.dma_start(w1n, w1).then_inc(s_ld["w1"], 16)
            sp.dma_start(xs[0][:, 0:NT // 2, :], x_v[0][:, 0:NT // 2, :]).then_inc(s_xf, 16)
            sp.dma_start(w2n, w2).then_inc(s_ld["w2"], 16)
            sp.dma_start(wk, mixw.rearrange("k o i a -> k o (i a)")).then_inc(s_ld["mixw"], 16)
            sp.dma_start(xs[0][:, NT // 2:NT, :], x_v[0][:, NT // 2:NT, :]).then_inc(s_x[0], 16)
            sp.dma_start(mbn, row(mixb, 1, BT)).then_inc(s_ld["mixb"], 16)
            for e in range(E0):
                sp.dma_start(bn[:, :, e * R0:(e + 1) * R0],
                             ffb[e].rearrange("(c p) r -> p c r", p=P)).then_inc(s_ld["bn"], 16)
            for g in range(C // CG):
                sp.dma_start(cwt[g * CG:(g + 1) * CG, :, :],
                             convw[g * CG:(g + 1) * CG].rearrange("o i k -> i o k")).then_inc(s_ld["conv"], 16)
            sp.dma_start(ctxn, ctxw).then_inc(s_ld["ctx"], 16)
            sp.dma_start(gw1n, gw1).then_inc(s_ld["gate"], 16)
            sp.dma_start(gw2n, row(gw2, 1, NT)).then_inc(s_ld["gate"], 16)
            sp.dma_start(xs[1][:, :, :], x_v[1]).then_inc(s_x[1], 16)
            sp.dma_start(lbn, lora_b.rearrange("e r h -> (e r) h")).then_inc(s_ld["lora"], 16)
            sp.dma_start(wn, wmain.rearrange("(c p) h -> p c h", p=P)).then_inc(s_ld["w"], 16)
            for e in range(E1):
                sp.dma_start(ga[:, :, G1 + e * R1:G1 + (e + 1) * R1],
                             lora_a[e].rearrange("(m q) r -> m q r", q=Q)).then_inc(s_ld["lora_a"], 16)
            wait(sp, s_cbias, 16)
            sp.dma_start(bias[0][:, :, :, :].rearrange("p t b c -> p (t b c)"),
                         cbias[0:NT * P].partition_broadcast(P)).then_inc(s_bias[0], 16)

            def step(s, par, k):
                if has(s, 0) and has(s, 2):
                    wait(sp, s_x1, s * NT + NT)
                    sp.dma_start(xs[par][:, :, :],
                                 x_v[bass.ds(s + 2, 1)].rearrange("s p t h -> p (s t) h")).then_inc(s_x[par], 16)
                if has(s, 0) and has(s, 1):
                    wait(sp, s_o1, s * NT)
                    sp.dma_start(bias[1 - par][:, :, :, :].rearrange("p t b c -> p (t b c)"),
                                 cbias[bass.ds((s + 1) * (NT * P), NT * P)].partition_broadcast(P))\
                      .then_inc(s_bias[1 - par], 16)
            steps(sp, step, -1, NS - 1)

            def store(s, par, k):
                for t in range(NT):
                    sp.wait_ge(s_yo[t], s + 1)
                    sp.dma_start(out_v[bass.ds(s * NT + t, 1)].rearrange("n p h -> p (n h)"), yo[par][t])\
                      .then_inc(s_out[par][t], 16)
            steps(sp, store, 0, NS - 1)
            for par in range(2):
                for t in range(NT):
                    sp.wait_ge(s_out[par][t], 16 * (NS // 2))

        @block.gpsimd
        def _(pool):
            pool.memset(ident[:, :], 0.0).then_inc(s_id, 1)
            pool.memset(ones[:, :], 1.0).then_inc(s_id, 1)
            pool.memset(repmask[:, :], 1.0).then_inc(s_id, 1)
            pool.memset(gq, 1.0).then_inc(s_id, 1)
            pool.memset(upper[:, :, :], 1.0).then_inc(s_id, 1)
            pool.wait_ge(s_id, 5)
            pool.affine_select(out=ident[:, :], in_=ident[:, :], compare_op=ALU.not_equal, fill=1.0, base=0,
                               pattern=[[-1, P]], channel_multiplier=1).then_inc(s_const, 1)
            pool.affine_select(out=repmask[:, :], in_=repmask[:, :], compare_op=ALU.is_ge, fill=0.0, base=0,
                               pattern=[[-C, BT]], channel_multiplier=1).then_inc(s_id, 1)
            pool.affine_select(out=gq, in_=gq, compare_op=ALU.is_ge, fill=0.0, base=0,
                               pattern=[[-C, BT], [-CG, C // CG]], channel_multiplier=1).then_inc(s_id, 1)
            pool.wait_ge(s_id, 7)
            pool.affine_select(out=repmask[:, :], in_=repmask[:, :], compare_op=ALU.is_ge, fill=0.0, base=C - 1,
                               pattern=[[C, BT]], channel_multiplier=-1).then_inc(s_const, 1)
            pool.affine_select(out=gq, in_=gq, compare_op=ALU.is_ge, fill=0.0, base=CG - 1,
                               pattern=[[C, BT], [CG, C // CG]], channel_multiplier=-1).then_inc(s_const, 1)
            pool.affine_select(out=upper[:, :, :], in_=upper[:, :, :], compare_op=ALU.is_gt, fill=0.0, base=0,
                               pattern=[[-1, E1], [1, E1]], channel_multiplier=0).then_inc(s_const, 1)
            pool.dma_start(b2b, b2.partition_broadcast(P)).then_inc(s_ld["b2"], 16)
            pool.dma_start(aw[0:ER0], ffa.rearrange("e r h -> (e r) h")).then_inc(s_ld["aw"], 16)
            pool.dma_start(aw[ER0:UC], ffr).then_inc(s_ld["aw"], 16)
            pool.dma_start(fsb, fside.partition_broadcast(P)).then_inc(s_ld["side"], 16)
            for e in range(E0):
                pool.memset(sel0[:, e:e + 1], 2.0 - e)
            for c in range(2):
                for e in range(E1):
                    pool.memset(sel1[:, c, e:e + 1], float(c - e))
            pool.memset(mhalf[:, :], -0.5)
            pool.memset(cnt[:, :, :], 0.0).then_inc(s_const, 1)
            pool.memset(taps, 0.0).then_inc(s_zero, 1)
            for i in range(2):
                pool.memset(xp[i][:, :, :, 0:1], 0.0)
                pool.memset(xp[i][:, :, :, M + 1:M + 2], 0.0).then_inc(s_zero, 1)
            pool.memset(gw2bd[:, :, :], 0.0).then_inc(s_zero, 1)

            def mixing(u):
                wait(pool, s_vp, u)
                pool.tensor_tensor(
                    mixbd[:, :, :, :],
                    mix_all[:, :, bass.ds(u * (NT * BT), NT * BT)].rearrange("p o (t r) -> p t r o", r=BT),
                    row(row(repmask[:, :], 1, NT), 3, C), ALU.mult).then_inc(s_bd, 1)
                if isinstance(u, int) and u == 0:
                    pool.wait_ge(s_ss["rs"], 1)
                wait(pool, s_v, u)
                pool.tensor_tensor(vb[:, :, :], row(mixbias[:, bass.ds(u * NT, NT)], 2, UC),
                                   row(rs[:, :], 1, NT), ALU.mult).then_inc(s_vb, 1)

            def rstd(u):
                pool.wait_ge(s_var, u + 1)
                pool.tensor_tensor(small[:, 16, :], small[:, 15, :], mhalf[:, :], ALU.pow).then_inc(s_rstd, 1)

            pool.wait_ge(s_ld["bn"], 16 * E0)
            pool.tensor_copy(bn2, row(bn, 2, 2)).then_inc(s_bn, 1)
            for d, src in ((gb1_b, gb1), (gamma_b, gamma), (beta_b, beta), (gb2_b, gb2)):
                pool.dma_start(d[:, :], src.partition_broadcast(P)).then_inc(s_ld["rows"], 16)
            pool.wait_ge(s_const, 5)
            pool.wait_ge(s_msa, MG // 2)
            pool.wait_ge(s_msd, MG // 2)
            pool.wait_ge(s_mbsb, 1)
            mixing(0)
            mixing(1)

            def step(s, par, k):
                if has(s, -1):
                    rstd(s - 1)
                if has(s, 2):
                    mixing(s + 2)
                if at_step(s, 0):
                    pool.wait_ge(s_gah, 1)
                    pool.tensor_tensor(wt_lo[:, :, H:H + GC], ga[:, :, :], wt_hi[:, :, H:H + GC].bitcast(fp32),
                                       ALU.subtract).then_inc(s_gal, 1)
                for t in range(NT):
                    if at_step(s, NS - 1) and t == NT - 1:
                        rstd(s)
                    pool.wait_ge(s_o1h, s * NT + t + 1)
                    pool.tensor_tensor(o1l[t % 2][:, :, :], o1[t % 2][:, :, :, :].rearrange("p q b c -> p q (b c)"),
                                       o1h[t % 2][:, :, :].bitcast(fp32), ALU.subtract).then_inc(s_o1l, 1)
            steps(pool, step, 0, NS - 1)

            def weigh(u, buffer):
                pool.wait_ge(s_w, 1 if at_step(u, 1) else 2)
                wait(pool, s_ltp, u - 1)
                pool.tensor_tensor(
                    ltw[buffer].rearrange("p (t e r) -> p t e r", t=NT, e=E1),
                    tmp_all[:, bass.ds(u * (NT * ER1), NT * ER1)].rearrange("p (t e r) -> p t e r", t=NT, e=E1),
                    row(wst_all[:, bass.ds(u * NT, NT), 0, :], 3, R1), ALU.mult).then_inc(s_lt, 1)

            def split(s, par, k):
                if has(s, 2):
                    weigh(s + 2, par)
                if has(s, 0) and has(s, 1):
                    pool.wait_ge(s_lth, s + 2)
                    wait(pool, s_lp, s * NT)
                    pool.tensor_tensor(lt_lo[1 - par][:, :], lt[1 - par][:, :], lt_hi[1 - par][:, :].bitcast(fp32),
                                       ALU.subtract).then_inc(s_ltl, 1)
            steps(pool, split, -1, NS - 1)

        @block.scalar
        def _(act):
            act.dma_start(b0c, b0.rearrange("(p a) -> p a", a=1)).then_inc(s_ld["b0"], 16)
            act.dma_start(b1c, b1.rearrange("(p a) -> p a", a=1)).then_inc(s_ld["b1"], 16)

            def x_transposed(u, tiles=range(NT)):
                for t in tiles:
                    act.wait_ge(s_xtp, u * NT + t + 1)
                    if t == 0:
                        wait(act, s_up, u)
                    nc.scalar.activation(xT[:, t, :, :].rearrange("p c m -> p (c m)"), ps_a[t % 2][:, :],
                                         ACT.Copy).then_inc(s_xt, 1)

            def u_out(u):
                act.wait_ge(s_up, u + 1)
                wait(act, s_vp, u)
                nc.scalar.activation(u_sb[:, :, :].rearrange("p t c -> p (t c)"), ps_a[0][:, 0:NT * UC],
                                     ACT.Copy).then_inc(s_u, 1)

            def gate0_exp(u):
                act.wait_ge(s_df0, u + 1)
                nc.scalar.activation(sc0[:, 1, :, :], sc0[:, 0, :, :], ACT.Exp).then_inc(s_ex0, 1)

            act.wait_ge(s_sp["h1"], 1)
            act.wait_ge(s_ld["b0"], 16)
            nc.scalar.activation(h1, ps_t[:, 0:P], ACT.Gelu, bias=b0c).then_inc(s_ss["h1"], 1)
            act.wait_ge(s_sp["h2"], 1)
            act.wait_ge(s_ld["b1"], 16)
            nc.scalar.activation(h2, ps_t[:, 0:P], ACT.Gelu, bias=b1c).then_inc(s_ss["h2"], 1)
            act.wait_ge(s_attd, 1)
            nc.scalar.activation(atte, att, ACT.Exp).then_inc(s_atte, 1)
            x_transposed(0, (0, 1))
            act.wait_ge(s_sp["mix0"], 1)
            nc.scalar.activation(mixn[:, 0:C // 2, :, :],
                                 row(ps_d[0][:, :].rearrange("p (o i) -> p o i", i=C), 2, BT), ACT.Copy)\
              .then_inc(s_ss["mix0"], 1)
            for g in range(0, MG, 2):
                act.wait_ge(s_mps, g + 1)
                nc.scalar.activation(mix_all[:, 4 * g:4 * g + 4, :].rearrange("p o b -> p (o b)"),
                                     ps_m[g % 4][:, :], ACT.Copy).then_inc(s_msa, 1)
                if g == 2:
                    x_transposed(0, (2, 3))
            u_out(0)
            x_transposed(1, (0, 1))
            gate0_exp(0)
            x_transposed(1, (2, 3))
            act.wait_ge(s_ss["ctx"], 1)
            act.dma_start(cbias.rearrange("(b c) -> b c", c=C), ctxb).then_inc(s_cbias, 16)

            def w_hi(q):
                act.wait_ge(s_wps, q + 1)
                nc.scalar.activation(wt_hi[:, q, 0:H].rearrange("p (q m) -> p q m", q=Q),
                                     ps_w[q][:, :].rearrange("p (m q) -> p q m", q=Q),
                                     ACT.Copy).then_inc(s_whi, 1)

            def step(s, par, k):
                def o_hi(t):
                    act.wait_ge(s_o1, s * NT + t + 1)
                    wait(act, s_mp, s * NT + max(t - 1, 0))
                    nc.scalar.activation(o1h[t % 2][:, :, :], o1[t % 2][:, :, :, :].rearrange("p q b c -> p q (b c)"),
                                         ACT.Copy).then_inc(s_o1h, 1)

                def ga_out(t):
                    if at_step(s, NS - 1):
                        act.wait_ge(s_gp, t + 1)
                        at = 0
                    else:
                        act.wait_ge(s_y, s * NT + t + 1)
                        at = H - MC
                    if t == 0:
                        wait(act, s_h, s)
                    nc.scalar.activation(hs[:, t, :], ps_g[:, at:at + G1], ACT.Copy)
                    nc.scalar.activation(tmp_all[:, bass.ds((s * NT + t) * ER1, ER1)], ps_g[:, at + G1:at + GC],
                                         ACT.Copy).then_inc(s_g, 1)

                def copies(n, base, first=0, tiles=NT):
                    for i in range(base, base + n):
                        to, source = shifted(i, s + 1, xp[1 - par], first, tiles)
                        last = nc.scalar.activation(to, source, ACT.Copy)
                    return last

                def gm_out():
                    act.wait_ge(s_gtp, s + 2)
                    wait(act, s_dp, (s + 1) * NT)
                    nc.scalar.activation(gmT[:, :], ps_t[:, :], ACT.Copy).then_inc(s_gt, 1)

                def gate1_exp():
                    act.wait_ge(s_df1, s)
                    nc.scalar.activation(sc1[:, 2, :, :], sc1[:, 1, :, :], ACT.Exp).then_inc(s_ex1, 1)

                if at_step(s, -1):
                    gm_out()
                    u_out(1)
                    act.wait_ge(s_x1, 2)
                    copies(BT * Q - EARLY_DVE, EARLY_DVE, 0, NT // 2).then_inc(s_xph, 1)
                    w_hi(0)
                    w_hi(1)
                    act.wait_ge(s_ss["gw1"], 1)
                    act.wait_ge(s_ld["lora_a"], 16 * E1)
                    nc.scalar.activation(wt_hi[:, :, H:H + GC], ga[:, :, :], ACT.Copy).then_inc(s_gah, 1)
                    act.wait_ge(s_x1, NT)
                    copies(BT * Q - EARLY_DVE, EARLY_DVE, NT // 2, NT // 2).then_inc(s_xpa, 1)
                    return
                if at_step(s, 0):
                    w_hi(2)
                    w_hi(3)
                    o_hi(0)
                    gate0_exp(1)
                    x_transposed(2, (0, 1))
                    gm_out()
                    x_transposed(2, (2, 3))
                else:
                    if has(s, 1):
                        gm_out()
                    if has(s, 2):
                        x_transposed(s + 2, (0,))
                    if has(s, 0):
                        o_hi(0)
                    if at_step(s, NS - 1):
                        ga_out(0)
                    if has(s, 2):
                        x_transposed(s + 2, (1, 2, 3))
                    if has(s, -1):
                        act.wait_ge(s_htp, s)
                        wait(act, s_rp, s - 1)
                        nc.scalar.activation(hT[:, :], ps_t[:, 0:P], ACT.Copy).then_inc(s_ht, 1)
                if has(s, -1) and not has(s, 1):
                    gate1_exp()
                if has(s, 1):
                    act.wait_ge(s_x1, (s + 1) * NT + NT)
                    wait(act, s_cp, s * NT)
                    copies(3, 8)
                if has(s, 0):
                    o_hi(1)
                if has(s, 1):
                    copies(3, 11)
                if at_step(s, NS - 1):
                    ga_out(1)
                elif has(s, 0):
                    ga_out(0)
                if has(s, -1) and has(s, 1):
                    gate1_exp()
                if has(s, 2):
                    u_out(s + 2)
                if at_step(s, NS - 1):
                    ga_out(2)
                    o_hi(2)
                    ga_out(3)
                    o_hi(3)
                    return
                if has(s, 0):
                    o_hi(2)
                if has(s, 2):
                    gate0_exp(s + 2)
                if has(s, 1):
                    copies(2, 14).then_inc(s_xpa, 1)
                if has(s, 0):
                    ga_out(1)
                if has(s, 0):
                    o_hi(3)
                    ga_out(2)
                    ga_out(3)
            steps(act, step, -1, NS)

            def split(s, par, k):
                if has(s, 1):
                    act.wait_ge(s_ltp, s + 2)
                    wait(act, s_lp, s * NT)
                    wait(act, s_ltl, s - 1)
                    last = nc.scalar.activation(lt_hi[1 - par][:, :], ps_a[1 - par][:, :], ACT.Copy)
                    if has(s, 0):
                        last = nc.scalar.activation(lt[1 - par][:, :], ps_a[1 - par][:, :], ACT.Copy)
                    last.then_inc(s_lth, 1)
            steps(act, split, -1, NS - 1)

        @block.vector
        def _(dve):
            link, n = chain(dve, s_sd, 0)
            V = nc.vector
            qm = "p (m q) -> p q m"
            mq = "p (q m) -> p q m"

            def gates0(u):
                link, n = chain(dve, s_c0, u * N_C0)
                dve.wait_ge(s_vp, u + 1)
                dve.wait_ge(s_vb, u + 1)
                V.tensor_tensor(v[:, :, :], ps_v[:, 0:NT * UC].rearrange("p (t c) -> p t c", t=NT), vb[:, :, :],
                                ALU.add).then_inc(s_v, 1)
                dve.wait_ge(s_v, u + 1)
                lg = v[:, :, ER0:UC]
                link(V.reduce_max(small[:, 0, :], lg, AXX))
                V.tensor_tensor(sc0[:, 0, :, :], lg, row(small[:, 0, :], 2, E0), ALU.subtract).then_inc(s_df0, 1)
                link(V.tensor_tensor(pair0[:, 0], row(lg, 2, E0), row(lg, 3, E0), ALU.is_gt))
                link(V.tensor_tensor(pair0[:, 1], pair0[:, 0], row(upper[:, 0:E0, 0:E0], 1, NT), ALU.mult))
                link(V.reduce_sum(sc0[:, 2], pair0[:, 1], AXX))
                link(V.reduce_sum(sc0[:, 3], pair0[:, 1].rearrange("p t e j -> p t j e"), AXX))
                link(V.tensor_tensor(sc0[:, 4], sc0[:, 2], sc0[:, 3], ALU.subtract))
                link(V.tensor_tensor(sc0[:, 5], sc0[:, 4], row(sel0[:, :], 1, NT), ALU.is_lt))
                dve.wait_ge(s_ex0, u + 1)
                link(V.tensor_tensor(sc0[:, 6], sc0[:, 1], sc0[:, 5], ALU.mult))
                link(V.reduce_sum(small[:, 1, :], sc0[:, 6], AXX))
                link(V.reciprocal(small[:, 2, :], small[:, 1, :]))
                link(V.scalar_tensor_tensor(out=sc0[:, 7], in0=sc0[:, 6], scalar=SCALE0,
                                            in1=row(small[:, 2, :], 2, E0), op0=ALU.mult, op1=ALU.mult))
                link(V.tensor_tensor(gm[:, :, :].rearrange("p t (e r) -> p t e r", e=E0),
                                     v[:, :, 0:ER0].rearrange("p t (e r) -> p t e r", e=E0),
                                     row(sc0[:, 7], 3, R0), ALU.mult))
                wait(dve, s_gtp, u)
                link(V.tensor_copy(gms[:, :, 0, :].bitcast(fp32r), gm[:, :, :]))
                V.tensor_tensor(gms[:, :, 1, :], gm[:, :, :], gms[:, :, 0, :], ALU.subtract).then_inc(s_gm, 1)
                assert n[0] == N_C0, n[0]

            dve.wait_ge(s_const, 3)
            V.tensor_reduce(gmask, gq.rearrange("p r g -> p g r"), axis=AXX, op=ALU.add)
            dve.wait_ge(s_sp["condT"], 1)
            V.tensor_copy(condT, ps_c[:, 0:P]).then_inc(s_ss["condT"], 1)
            dve.wait_ge(s_sp["att"], 1)
            dve.wait_ge(s_ld["b2"], 16)
            link(V.tensor_tensor(att, ps_t[:, 0:K0], b2b, ALU.add))
            link(V.reduce_max(sm[:, 0:1], att, AXX))
            V.tensor_scalar(att, att, sm[:, 0:1], None, ALU.subtract).then_inc(s_attd, 1)
            dve.wait_ge(s_atte, 1)
            link(V.reduce_sum(sm[:, 1:2], atte, AXX))
            link(V.reciprocal(sm[:, 2:3], sm[:, 1:2]))
            V.tensor_scalar(att, atte, sm[:, 2:3], None, ALU.mult).then_inc(s_ss["att"], 1)
            dve.wait_ge(s_sp["attT"], 1)
            V.tensor_copy(attT, ps_v[0:K0, 0:P]).then_inc(s_ss["attT"], 1)
            dve.wait_ge(s_ld["conv"], 16 * (C // CG))
            dve.wait_ge(s_zero, 1)
            for q in range(Q):
                last = V.tensor_copy(taps[C * q:C * q + C, :, Q - 1 - q:Q - 1 - q + TAPS], cwt)
            link(last)
            for j in range(SH):
                for p in range(Q):
                    last = V.tensor_tensor(cw[:, j, p, :].rearrange("i (g o) -> i g o", o=CG),
                                           row(taps[:, :, Q * j - p + Q - 1], 1, C // CG), row(gmask, 2, CG), ALU.mult)
            last.then_inc(s_cw, 1)
            dve.wait_ge(s_sp["pm"], 1)
            V.tensor_copy(pm[:, :, :].rearrange("p c u -> p (c u)"), ps_c[:, 0:HC * UC]).then_inc(s_ss["pm"], 1)
            dve.wait_ge(s_sp["mix1"], 1)
            V.tensor_copy(mixn[:, C // 2:C, :, :], row(ps_d[1][:, :].rearrange("p (o i) -> p o i", i=C), 2, BT))\
             .then_inc(s_ss["mix1"], 1)
            dve.wait_ge(s_mbps, 1)
            for r in range(BT):
                last = V.tensor_copy(mixbias[C * r:C * r + C, :],
                                     ps_v[C * r:C * r + C, 128:128 + NB].rearrange("p (n r) -> p n r", r=BT)[:, :, r])
            last.then_inc(s_mbsb, 1)
            for g in range(1, MG, 2):
                dve.wait_ge(s_mps, g + 1)
                V.tensor_copy(mix_all[:, 4 * g:4 * g + 4, :].rearrange("p o b -> p (o b)"),
                              ps_m[g % 4][:, :]).then_inc(s_msd, 1)
            dve.wait_ge(s_sp["gw1"], 1)
            dve.wait_ge(s_zero, 4)
            for t in range(NT):
                V.tensor_copy(gw2bd[G1 * t:G1 * t + G1, t, :], ps_v[G1 * t:G1 * t + G1, GWC + Q * G1:GWC + Q * G1 + E1])
            V.tensor_copy(ga[:, :, 0:G1], ps_v[:, GWC:GWC + Q * G1].rearrange("p (q g) -> p q g", q=Q))\
             .then_inc(s_ss["gw1"], 1)
            dve.wait_ge(s_sp["b"], 1)
            link(V.tensor_copy(b_hi[:, :].rearrange(mq, q=Q), ps_t[:, :].rearrange(qm, q=Q)))
            V.tensor_tensor(b_lo[:, :].rearrange(mq, q=Q), ps_t[:, :].rearrange(qm, q=Q),
                            b_hi[:, :].bitcast(fp32).rearrange(mq, q=Q), ALU.subtract).then_inc(s_ss["b"], 1)
            dve.wait_ge(s_ld["lora"], 16)
            link(V.tensor_copy(lb_hi[:, :].rearrange(mq, q=Q), lbn.rearrange(qm, q=Q)))
            V.tensor_tensor(lb_lo[:, :].rearrange(mq, q=Q), lbn.rearrange(qm, q=Q),
                            lb_hi[:, :].bitcast(fp32).rearrange(mq, q=Q), ALU.subtract).then_inc(s_lb, 1)
            dve.wait_ge(s_sp["rs"], 1)
            V.tensor_copy(rs[:, :], ps_c[:, 0:UC]).then_inc(s_ss["rs"], 1)
            dve.wait_ge(s_sp["ctxT"], 1)
            V.tensor_copy(ctxT, ps_g[:, 0:C]).then_inc(s_ss["ctxT"], 1)
            gates0(0)
            dve.wait_ge(s_sp["ctx"], 1)
            dve.wait_ge(s_ld["side"], 16)
            V.tensor_tensor(ctxb, ps_g[:, 0:C], fsb, ALU.add).then_inc(s_ss["ctx"], 1)
            dve.wait_ge(s_ld["rows"], 16 * 4)

            def y_out(u, t):
                if at_step(u, NS - 1):
                    dve.wait_ge(s_mp, u * NT + t + 1)
                    yt = y_all[:, bass.ds(u * ST + t * H, H)]
                    V.tensor_tensor(yt, ps_d[t % 2][:, :], yt, ALU.add).then_inc(s_y, 1)
                else:
                    dve.wait_ge(s_ma, u * NT + t + 1)
                    yt = y_all[:, bass.ds(u * ST + t * H, MC)]
                    V.tensor_tensor(yt, ps_d[t % 2][:, 0:MC], yt, ALU.add)
                    dve.wait_ge(s_mp, u * NT + t + 1)
                    yt = y_all[:, bass.ds(u * ST + t * H + MC, H - MC)]
                    V.tensor_tensor(yt, ps_g[:, 0:H - MC], yt, ALU.add).then_inc(s_y, 1)

            def w_lo(q):
                dve.wait_ge(s_whi, q + 1)
                V.tensor_tensor(wt_lo[:, q, 0:H].rearrange(mq, q=Q), ps_w[q][:, :].rearrange(qm, q=Q),
                                wt_hi[:, q, 0:H].bitcast(fp32).rearrange(mq, q=Q), ALU.subtract).then_inc(s_wlo, 1)

            def choices(u):
                link, n = chain(dve, s_c2, u * N_C2)
                dve.wait_ge(s_rp, u + 1)
                V.tensor_tensor(sc1[:, 0], ps_v[:, 0:NT * E1].rearrange("p (t e) -> p t e", t=NT),
                                row(gb2_b[:, :], 1, NT), ALU.add).then_inc(s_r, 1)
                dve.wait_ge(s_r, u + 1)
                link(V.tensor_tensor(pair1[:, :, :, :], row(sc1[:, 0], 2, E1), row(sc1[:, 0], 3, E1), ALU.is_gt), False)
                link(V.reduce_max(small[:, 4, :], sc1[:, 0], AXX))
                link(V.tensor_tensor(pair1[:, :, :, :], pair1[:, :, :, :], row(upper[:, :, :], 1, NT), ALU.mult), False)
                V.tensor_tensor(sc1[:, 1], sc1[:, 0], row(small[:, 4, :], 2, E1), ALU.subtract).then_inc(s_df1, 1)
                dve.wait_ge(s_c2, u * N_C2 + n[0])
                link(V.reduce_sum(sc1[:, 3], pair1[:, :, :, :], AXX), False)
                link(V.reduce_sum(sc1[:, 4], pair1[:, :, :, :].rearrange("p t e j -> p t j e"), AXX))
                link(V.tensor_tensor(sc1[:, 5], sc1[:, 3], sc1[:, 4], ALU.subtract))
                chosen = V.tensor_tensor(oh[:, :, :, :], row(sc1[:, 5], 2, 2), row(sel1[:, :, :], 1, NT), ALU.is_equal)
                if at_step(u, NS - 1):
                    chosen.then_inc(s_cnt, 1)
                    dve.wait_ge(s_cnt, 1)
                else:
                    link(chosen)
                    link(V.reduce_sum(cnt1[:, :, :], oh[:, :, :, :].rearrange("p t c e -> p c e t"), AXX), False)
                dve.wait_ge(s_ex1, u + 1)
                link(V.tensor_tensor(exs1[:, :, :, :], row(sc1[:, 2], 2, 2), oh[:, :, :, :], ALU.mult))
                if not at_step(u, NS - 1):
                    link(V.tensor_tensor(cnt[:, :, :], cnt[:, :, :], cnt1[:, :, :], ALU.add), False)
                exf = exs1[:, :, :, :].rearrange("p t c e -> p t (c e)")
                link(V.reduce_sum(small[:, 5, :], exf, AXX))
                link(V.reciprocal(small[:, 6, :], small[:, 5, :]))
                link(V.scalar_tensor_tensor(
                    out=wst_all[:, bass.ds(u * NT, NT), :, :].rearrange("p t c e -> p t (c e)"), in0=exf,
                    scalar=ALPHA, in1=row(small[:, 6, :], 2, 2 * E1), op0=ALU.mult, op1=ALU.mult))
                assert at_step(u, NS - 1) or n[0] == N_C2, n[0]

            def norm_first(u):
                link, n = chain(dve, s_c1, u * N_C1)
                dve.wait_ge(s_g, u * NT + NT)
                link(V.tensor_tensor(ha[:, :, :], hs[:, :, :], row(gb1_b[:, :], 1, NT), ALU.add))
                link(V.reduce_sum(small[:, 12, :], ha[:, :, :], AXX))
                link(V.scalar_tensor_tensor(out=hb[:, :, :], in0=row(small[:, 12, :], 2, G1), scalar=-1.0 / G1,
                                            in1=ha[:, :, :], op0=ALU.mult, op1=ALU.add))
                link(V.tensor_tensor(ha[:, :, :], hb[:, :, :], hb[:, :, :], ALU.mult))
                link(V.reduce_sum(small[:, 14, :], ha[:, :, :], AXX))
                V.tensor_scalar(small[:, 15, :], small[:, 14, :], 1.0 / G1, EPS, ALU.mult, ALU.add)\
                 .then_inc(s_var, 1)
                link(V.tensor_tensor(ha[:, :, :], hb[:, :, :], row(gamma_b[:, :], 1, NT), ALU.mult), False)
                assert n[0] == N_C1A, n[0]

            def norm_last(u):
                link, n = chain(dve, s_c1, u * N_C1 + N_C1A)
                dve.wait_ge(s_c1, u * N_C1 + N_C1A)
                dve.wait_ge(s_rstd, u + 1)
                link(V.tensor_tensor(hb[:, :, :], ha[:, :, :], row(small[:, 16, :], 2, G1), ALU.mult))
                link(V.tensor_tensor(ha[:, :, :], hb[:, :, :], row(beta_b[:, :], 1, NT), ALU.add))
                wait(dve, s_htp, u)
                V.tensor_scalar(hr[:, :, :], ha[:, :, :], 0.0, None, ALU.max).then_inc(s_h, 1)
                assert n[0] == N_C1 - N_C1A, n[0]

            def step(s, par, k):
                def o_out(t):
                    dve.wait_ge(s_cp, s * NT + t + 1)
                    if at_step(s, NS - 1):
                        wait(dve, s_gp, t - 1)
                    wait(dve, s_o1l, s * NT + max(t - 1, 0))
                    if t == 0:
                        dve.wait_ge(s_bias[par], 16 * (k + 1))
                    V.tensor_tensor(o1[t % 2][:, :, :, :].rearrange("m p b o -> m b p o"),
                                    ps_c[:, :].rearrange("m (b p o) -> m b p o", b=BT, p=Q),
                                    row(bias[par][:, t, :, :], 2, Q), ALU.add).then_inc(s_o1, 1)

                def x1_out(t):
                    dve.wait_ge(s_dp, (s + 1) * NT + t + 1)
                    V.tensor_tensor(y_all[:, bass.ds((s + 1) * ST + t * H, H)].rearrange("p (q m) -> p q m", q=Q),
                                    ps_d[t % 2][:, :].rearrange("p (q m) -> p q m", q=Q),
                                    xs[1 - par][:, t, :].rearrange("p (m q) -> p q m", q=Q), ALU.add)\
                     .then_inc(s_x1, 1)

                def copies(n, base, first=0, tiles=NT):
                    for i in range(base, base + n):
                        to, source = shifted(i, s + 1, xp[1 - par], first, tiles)
                        last = V.tensor_scalar(to, source, 1.0, None, ALU.mult)
                    return last

                if at_step(s, -1):
                    x1_out(0)
                    x1_out(1)
                    dve.wait_ge(s_x1, 2)
                    copies(EARLY_DVE, 0, 0, NT // 2).then_inc(s_xph, 1)
                    x1_out(2)
                    x1_out(3)
                    w_lo(0)
                    w_lo(1)
                    return
                if at_step(s, NS - 1):
                    o_out(0)
                if has(s, -1) and has(s, 0):
                    norm_first(s - 1)
                if has(s, 0) and has(s, 1):
                    o_out(0)
                if has(s, -1) and has(s, 1):
                    x1_out(0)
                if has(s, -1) and has(s, 0):
                    norm_last(s - 1)
                if at_step(s, 0):
                    gates0(1)
                    w_lo(2)
                    w_lo(3)
                    o_out(1)
                if at_step(s, NS - 1):
                    o_out(1)
                if has(s, -1) and not has(s, 1):
                    choices(s - 1)
                if has(s, 1):
                    for t in range(1 if has(s, -1) else 0, NT):
                        if at_step(s, NS - 2) and t == 2:
                            o_out(1)
                        x1_out(t)
                    if at_step(s, 0):
                        for i in range(EARLY_DVE):
                            to, source = shifted(i, 0, xp[0], NT // 2, NT // 2)
                            last = V.tensor_scalar(to, source, 1.0, None, ALU.mult)
                        last.then_inc(s_xpd, 1)
                    dve.wait_ge(s_x1, (s + 1) * NT + NT)
                    wait(dve, s_cp, s * NT)
                    copies(2, 0)
                if has(s, 0) and has(s, 2) and not at_step(s, 0):
                    o_out(1)
                if has(s, 1):
                    copies(3, 2)
                if has(s, 0) and has(s, 1):
                    y_out(s, 0)
                if has(s, -1) and has(s, 1):
                    choices(s - 1)
                if has(s, 0):
                    o_out(2)
                if has(s, 2):
                    gates0(s + 2)
                if has(s, 1):
                    copies(3, 5).then_inc(s_xpd, 1)
                    y_out(s, 1)
                if has(s, 0):
                    o_out(3)
                    y_out(s, 2 if has(s, 1) else 0)
                    if has(s, 1):
                        y_out(s, 3)
                    else:
                        norm_first(s)
                        y_out(s, 1)
                        norm_last(s)
            steps(dve, step, -1, NS)

            link, n = chain(dve, s_c3, 0)
            dve.wait_ge(s_cntp, 1)
            link(V.tensor_scalar(allowed[:, :, :], ps_g[:, 0:2 * E1].rearrange("p (c e) -> p c e", c=2),
                                 float(CAPACITY), None, ALU.is_le))

            def allow(first, last):
                part = wst_all[:, first * NT:last * NT]
                link(V.tensor_tensor(part, part, row(allowed[:, :, :], 1, (last - first) * NT), ALU.mult))
                return V.tensor_tensor(part[:, :, 0, :], part[:, :, 0, :], part[:, :, 1, :], ALU.add)

            link(allow(0, 1))
            V.tensor_tensor(ltw[0].rearrange("p (t e r) -> p t e r", t=NT, e=E1),
                            tmp_all[:, 0:NT * ER1].rearrange("p (t e r) -> p t e r", t=NT, e=E1),
                            row(wst_all[:, 0:NT, 0, :], 3, R1), ALU.mult).then_inc(s_lt, 1)
            allow(1, 2).then_inc(s_w, 1)
            allow(2, NS).then_inc(s_w, 1)
            y_out(NS - 1, 2)
            y_out(NS - 1, 3)
            dve.wait_ge(s_lth, 1)
            V.tensor_tensor(lt_lo[0][:, :], ps_a[0][:, :], lt_hi[0][:, :].bitcast(fp32), ALU.subtract)\
             .then_inc(s_ltf, 1)

            dve.wait_ge(s_y, NS * NT)

            def finish(s, par, k):
                if has(s, 0):
                    for t in range(NT):
                        dve.wait_ge(s_lp, s * NT + t + 1)
                        wait(dve, s_out[par][t], k * 16)
                        V.tensor_tensor(yo[par][t].rearrange(qm, q=Q), ps_l[t][:, :].rearrange(mq, q=Q),
                                        y_all[:, bass.ds(s * ST + t * H, H)].rearrange(mq, q=Q),
                                        ALU.add).then_inc(s_yo[t], 1)
            steps(dve, finish, 0, NS - 1)

        @block.tensor
        def _(pe):
            T = nc.tensor
            idp = ident[:, :]

            def t1(u, bank_x, t):
                for c in range(HC):
                    last = T.transpose(ps_a[t % 2][:, c * P:(c + 1) * P], bank_x[:, t, c * P:(c + 1) * P], idp)
                last.then_inc(s_xtp, 1)

            def u_products(u, tiles=range(NT)):
                if tiles[0] == 0:
                    pe.wait_ge(s_xt, u * NT + NT - 1)
                for t in tiles:
                    if t == NT - 1:
                        pe.wait_ge(s_xt, u * NT + NT)
                    for c in range(HC):
                        last = T.matmul(ps_a[0][:, t * UC:(t + 1) * UC], xT[:, t, c, :], pm[:, c, :],
                                        start=(c == 0), stop=(c == HC - 1))
                if tiles[-1] == NT - 1:
                    last.then_inc(s_up, 1)

            def mix(u):
                pe.wait_ge(s_u, u + 1)
                pe.wait_ge(s_bd, u + 1)
                wait(pe, s_v, u)
                wait(pe, s_r, u - 2)
                for t in range(NT):
                    last = T.matmul(ps_v[:, t * UC:(t + 1) * UC],
                                    mixbd[:, t, :, :].rearrange("p r o -> p (r o)"), u_sb[:, t, :],
                                    start=True, stop=True)
                last.then_inc(s_vp, 1)

            def main(u, t, phases=range(Q)):
                if phases[0] == 0:
                    pe.wait_ge(s_o1l, u * NT + t + 1)
                    if t < 2 and has(u, 1):
                        pe.wait_ge(s_x1, (u + 1) * NT + 3 + t)
                    else:
                        wait(pe, s_y, u * NT + t - 1)

                def product(bank, first, columns):
                    for q in phases:
                        for n, (a, w) in enumerate(((o1h, wt_hi), (o1h, wt_lo), (o1l, wt_hi))):
                            last = T.matmul(bank[:, 0:columns], a[t % 2][:, q, :], w[:, q, first:first + columns],
                                            start=(q == 0 and n == 0), stop=(q == Q - 1 and n == 2))
                    return last

                if at_step(u, NS - 1):
                    last = product(ps_d[t % 2], 0, H)
                else:
                    if at_step(u, 0) and t == 0:
                        pe.wait_ge(s_gal, 1)
                    product(ps_d[t % 2], 0, MC).then_inc(s_ma, 1)
                    wait(pe, s_y, u * NT + t)
                    wait(pe, s_g, u * NT + t)
                    last = product(ps_g, MC, MC)
                if phases[-1] == Q - 1:
                    last.then_inc(s_mp, 1)

            pe.wait_ge(s_const, 1)
            pe.wait_ge(s_ld["cond"], 16)
            T.transpose(ps_c[:, 0:P], condn, idp).then_inc(s_sp["condT"], 1)
            pe.wait_ge(s_ld["w0"], 16)
            pe.wait_ge(s_ss["condT"], 1)
            T.matmul(ps_t[:, 0:P], w0n, condT, start=True, stop=True).then_inc(s_sp["h1"], 1)
            pe.wait_ge(s_ld["w1"], 16)
            pe.wait_ge(s_ss["h1"], 1)
            T.matmul(ps_t[:, 0:P], w1n, h1, start=True, stop=True).then_inc(s_sp["h2"], 1)
            pe.wait_ge(s_ld["w2"], 16)
            pe.wait_ge(s_ss["h2"], 1)
            T.matmul(ps_t[:, 0:K0], h2, w2n, start=True, stop=True).then_inc(s_sp["att"], 1)
            pe.wait_ge(s_xf, 16)
            t1(0, xs[0], 0)
            t1(0, xs[0], 1)
            pe.wait_ge(s_ss["att"], 1)
            T.transpose(ps_v[0:K0, 0:P], att, idp).then_inc(s_sp["attT"], 1)
            pe.wait_ge(s_ld["aw"], 32)
            for c in range(HC):
                last = T.transpose(ps_c[:, c * UC:(c + 1) * UC], aw[:, c * P:(c + 1) * P], ident[0:UC, 0:UC])
            last.then_inc(s_sp["pm"], 1)
            pe.wait_ge(s_ss["attT"], 1)
            pe.wait_ge(s_ld["mixw"], 16)
            for i in range(2):
                T.matmul(ps_d[i][:, :], attT, wk[:, i * (C // 2):(i + 1) * (C // 2), :].rearrange("k o i -> k (o i)"),
                         start=True, stop=True).then_inc(s_sp[f"mix{i}"], 1)
            pe.wait_ge(s_ld["mixb"], 16)
            T.matmul(ps_v[:, P:P + NB], mbn.rearrange("k r o -> k (r o)"), attT, start=True, stop=True)\
             .then_inc(s_mbps, 1)
            pe.wait_ge(s_bn, 1)
            for c in range(HC):
                last = T.transpose(ps_t[:, c * P:(c + 1) * P], bn2[:, c, :, :].rearrange("p d e -> p (d e)"), idp)
            last.then_inc(s_sp["b"], 1)
            for g in range(MG):
                if g < 4:
                    pe.wait_ge(s_ss[("pm", "condT", "mix0", "mix1")[g]], 1)
                elif g % 2 == 0:
                    pe.wait_ge(s_msa, g // 2 - 1)
                else:
                    pe.wait_ge(s_msd, g // 2 - 1)
                pe.wait_ge(s_ss["mix0" if g < MG // 2 else "mix1"], 1)
                for o in range(4):
                    last = T.transpose(ps_m[g % 4][:, o * NB:(o + 1) * NB],
                                       mixn[:, 4 * g + o, :, :].rearrange("b r i -> b (r i)"), idp)
                last.then_inc(s_mps, 1)
                if g == 3:
                    pe.wait_ge(s_x[0], 16)
                    for t in (2, 3):
                        pe.wait_ge(s_xt, t - 1)
                        t1(0, xs[0], t)
            pe.wait_ge(s_ld["gate"], 32)
            pe.wait_ge(s_mbsb, 1)
            for q in range(Q):
                last = T.transpose(ps_v[:, GWC + q * G1:GWC + (q + 1) * G1],
                                   gw1n.rearrange("p (m q) -> p q m", q=Q)[:, q, :], ident[0:G1, 0:G1])
            T.transpose(ps_v[:, GWC + Q * G1:GWC + Q * G1 + E1], gw2n.rearrange("e t c -> e (t c)"),
                        ident[0:E1, 0:E1]).then_inc(s_sp["gw1"], 1)
            u_products(0)
            pe.wait_ge(s_msa, 3)
            for c in range(HC):
                last = T.matmul(ps_c[:, 0:UC], ones[:, :], pm[:, c, :], start=(c == 0), stop=(c == HC - 1))
            last.then_inc(s_sp["rs"], 1)
            pe.wait_ge(s_msd, 3)
            pe.wait_ge(s_ld["ctx"], 16)
            T.transpose(ps_g[:, 0:C], ctxn, ident[0:C, 0:C]).then_inc(s_sp["ctxT"], 1)
            pe.wait_ge(s_ss["gw1"], 1)
            mix(0)
            pe.wait_ge(s_ss["ctxT"], 1)
            T.matmul(ps_g[:, 0:C], condT, ctxT, start=True, stop=True).then_inc(s_sp["ctx"], 1)
            pe.wait_ge(s_x[1], 16)
            for t in range(NT):
                if t == 0:
                    pe.wait_ge(s_u, 1)
                pe.wait_ge(s_xt, NT + max(t - 1, 0))
                t1(1, xs[1], t)
            u_products(1, (0, 1))

            def step(s, par, k):
                def conv(t):
                    if t == 0 and at_step(s, 0):
                        pe.wait_ge(s_xph, 2)
                    elif t == (2 if at_step(s, 0) else 0):
                        pe.wait_ge(s_xpd, s + 1)
                        pe.wait_ge(s_xpa, s + 1)
                    wait(pe, s_o1, s * NT + t)
                    for b in range(BT):
                        for j in range(SH):
                            last = T.matmul(ps_c[:, b * P:(b + 1) * P], xp[par][:, b, t, j:j + M],
                                            cw[:, j, :, :].rearrange("p q o -> p (q o)"),
                                            start=(j == 0), stop=(j == SH - 1))
                    last.then_inc(s_cp, 1)

                def gates(t):
                    pe.wait_ge(s_o1, s * NT + t + 1)
                    wait(pe, s_g, s * NT + t)
                    wait(pe, s_y, s * NT)
                    for q in range(Q):
                        last = T.matmul(ps_g[:, 0:GC], o1[t % 2][:, q, :, :].rearrange("p b c -> p (b c)"),
                                        ga[:, q, :], start=(q == 0), stop=(q == Q - 1))
                    last.then_inc(s_gp, 1)

                def delta(t):
                    if t < 2:
                        wait(pe, s_y, s * NT)
                        wait(pe, s_x1, s * NT + NT)
                    else:
                        pe.wait_ge(s_x1, (s + 1) * NT + t - 1)
                    lhs = gmT[:, t * P:(t + 1) * P]
                    T.matmul(ps_d[t % 2][:, :], lhs, b_hi[:, :], start=True, stop=False)
                    T.matmul(ps_d[t % 2][:, :], lhs, b_lo[:, :], start=False, stop=True).then_inc(s_dp, 1)

                def x_transposed(t):
                    if t == 0:
                        pe.wait_ge(s_x[par], 16 * (k + 2))
                        pe.wait_ge(s_u, s + 2)
                    wait(pe, s_xt, (s + 2) * NT + max(t - 1, 0))
                    t1(s + 2, xs[par], t)

                ahead = has(s, 0) and has(s, 2)

                def w_transposed(q):
                    if q == 0:
                        pe.wait_ge(s_ld["w"], 16)
                        pe.wait_ge(s_u, 2)
                    elif q == 1:
                        pe.wait_ge(s_xt, 2 * NT)
                    else:
                        pe.wait_ge(s_x1, NT - 3 + q)
                    for c in range(HC):
                        last = T.transpose(ps_w[q][:, c * P:(c + 1) * P],
                                           wn[:, c, :].rearrange("p (m q) -> p q m", q=Q)[:, q, :], idp)
                    last.then_inc(s_wps, 1)

                def gm_transposed():
                    pe.wait_ge(s_gm, s + 2)
                    wait(pe, s_ht, s - 1)
                    for t in range(NT):
                        last = T.transpose(ps_t[:, t * P:(t + 1) * P],
                                           gms[:, t, :, :].rearrange("p a c -> p (a c)"), idp)
                    last.then_inc(s_gtp, 1)

                def hidden_transposed():
                    pe.wait_ge(s_h, s)
                    pe.wait_ge(s_gt, upto(s + 2, NS))
                    T.transpose(ps_t[:, 0:P], hr[:, :, :].rearrange("p t g -> p (t g)"), idp).then_inc(s_htp, 1)

                def router():
                    pe.wait_ge(s_ht, s)
                    pe.wait_ge(s_v, upto(s + 2, NS))
                    T.matmul(ps_v[:, 0:NT * E1], hT[:, :], gw2bd[:, :, :].rearrange("p t e -> p (t e)"),
                             start=True, stop=True).then_inc(s_rp, 1)

                if at_step(s, 0):
                    pe.wait_ge(s_cw, 1)
                    pe.wait_ge(s_zero, 4)
                    conv(0)
                    w_transposed(2)
                    w_transposed(3)
                    conv(1)
                    pe.wait_ge(s_wlo, 2)
                    x_transposed(0)
                    x_transposed(1)
                    gm_transposed()
                    x_transposed(2)
                    pe.wait_ge(s_gt, 2)
                    pe.wait_ge(s_wlo, Q)
                    delta(0)
                    delta(1)
                    x_transposed(3)
                    delta(2)
                    delta(3)
                else:
                    if has(s, 1):
                        gm_transposed()
                    if has(s, 0):
                        conv(0)
                    if ahead:
                        x_transposed(0)
                    if at_step(s, NS - 1):
                        gates(0)
                    if at_step(s, -1):
                        u_products(1, (2,))
                    if has(s, 1):
                        pe.wait_ge(s_gt, s + 2)
                        delta(0)
                        delta(1)
                    if at_step(s, NS - 2):
                        conv(1)
                    if at_step(s, -1):
                        u_products(1, (3,))
                    if ahead:
                        x_transposed(1)
                    if has(s, 1):
                        delta(2)
                    if ahead:
                        x_transposed(2)
                        x_transposed(3)
                    if has(s, 1):
                        delta(3)
                    if has(s, -1) and not at_step(s, NS - 1):
                        hidden_transposed()
                    if has(s, 0) and not at_step(s, NS - 2):
                        conv(1)
                    if at_step(s, NS - 1):
                        hidden_transposed()
                    if at_step(s, NS):
                        main(NS - 1, 2, (3,))
                    if has(s, -1) and not at_step(s, NS - 1):
                        router()
                if at_step(s, NS):
                    main(NS - 1, 3, (0, 1))
                if at_step(s, NS - 1):
                    main(s, 0, (0, 1))
                    router()
                    gates(1)
                    conv(2)
                    main(s, 0, (2,))
                    gates(2)
                    conv(3)
                    main(s, 0, (3,))
                    gates(3)
                    main(s, 1)
                    main(s, 2, (0, 1, 2))
                    return
                if has(s, 0):
                    main(s, 0)
                if ahead:
                    u_products(s + 2)
                if has(s, 0):
                    conv(2)
                if has(s, 2):
                    mix(s + 2)
                if has(s, 0):
                    main(s, 1)
                if at_step(s, -1):
                    w_transposed(0)
                    w_transposed(1)
                if has(s, 0):
                    conv(3)
                    main(s, 2)
                    main(s, 3)
            steps(pe, step, -1, NS)

            pe.wait_ge(s_c2, (NS - 1) * N_C2)
            T.matmul(ps_g[:, 0:2 * E1], ones[:, :], cnt[:, :, :].rearrange("p c e -> p (c e)"), start=True, stop=False)
            pe.wait_ge(s_cnt, 1)
            for t in range(NT):
                last = T.matmul(ps_g[:, 0:2 * E1], ones[:, :], oh[:, t, :, :].rearrange("p c e -> p (c e)"),
                                start=False, stop=(t == NT - 1))
            last.then_inc(s_cntp, 1)
            main(NS - 1, 3, (2, 3))
            pe.wait_ge(s_lb, 1)

            def lora(s, par, k):
                def weighted_transposed():
                    pe.wait_ge(s_lt, s + 2)
                    wait(pe, s_lth, s)
                    for t in range(NT):
                        last = T.transpose(ps_a[1 - par][:, t * P:(t + 1) * P],
                                           ltw[1 - par][:, t * P:(t + 1) * P], idp)
                    last.then_inc(s_ltp, 1)

                def high(t):
                    wait(pe, s_yo[t], s)
                    lhs = lt_hi[par][:, t * P:(t + 1) * P]
                    T.matmul(ps_l[t][:, :], lhs, lb_hi[:, :], start=True, stop=False)
                    T.matmul(ps_l[t][:, :], lhs, lb_lo[:, :], start=False, stop=False)

                def low(t):
                    T.matmul(ps_l[t][:, :], lt_lo[par][:, t * P:(t + 1) * P], lb_hi[:, :],
                             start=False, stop=True).then_inc(s_lp, 1)

                if at_step(s, 0):
                    weighted_transposed()
                    pe.wait_ge(s_lth, 1)
                    high(0)
                    high(1)
                    pe.wait_ge(s_ltf, 1)
                    low(0)
                    low(1)
                    pe.wait_ge(s_y, NS * NT)
                    for t in (2, 3):
                        high(t)
                        low(t)
                    return
                if has(s, 1):
                    weighted_transposed()
                if has(s, 0):
                    pe.wait_ge(s_ltl, s)
                    for t in range(NT):
                        high(t)
                        low(t)
            steps(pe, lora, -1, NS - 1)


_INS = ['x', 'cond_128', 'fside_S_0', 'L0_cond_W0', 'L0_cond_b0', 'L0_cond_W1', 'L0_cond_b1', 'L0_cond_W2',
        'L0_cond_b2', 'L0_cond_weight', 'L0_cond_bias_k', 'L0_ffn_A', 'L0_ffn_B', 'L0_ffn_Wr', 'L1_cond_weight',
        'L1_cond_c_weight', 'L1_ffn_weight', 'L1_ffn_lora_A', 'L1_ffn_lora_B', 'L1_ffn_gw1', 'L1_ffn_gb1',
        'L1_ffn_ln_gamma', 'L1_ffn_ln_beta', 'L1_ffn_gw2', 'L1_ffn_gb2']


def kernel(**inputs):
    import numpy as _np
    import concourse.bacc as _bacc
    from concourse import mybir as _mybir
    from concourse.bass_utils import run_bass_kernel_spmd as _run

    nc = _bacc.Bacc("TRN2", target_bir_lowering=False, num_devices=1)
    arrays, args = {}, []
    for name in _INS:
        a = _np.ascontiguousarray(inputs[name])
        arrays[f"in_{name}_dram"] = a
        args.append(nc.dram_tensor(f"in_{name}_dram", a.shape, _mybir.dt.from_np(a.dtype), kind="ExternalInput").ap())
    shape = _np.shape(inputs['x'])
    args.append(nc.dram_tensor("out_dram", shape, _mybir.dt.float32, kind="ExternalOutput").ap())
    adaln_ffn_kernel(nc, *args)
    r = _run(nc, [arrays], core_ids=[0])
    return r.results[0]["out_dram"]
```
